# Optimizing a Trainium2 kernel written in Bass

```python
import numpy as np
import jax
import jax.numpy as jnp

def _softmax(x, axis=-1):
    return jax.nn.softmax(x, axis=axis)

def _gelu(x):
    return jax.nn.gelu(x, approximate=True)

def _silu(x):
    return jax.nn.silu(x)

def _sigmoid(x):
    return jax.nn.sigmoid(x)

def _layernorm(x, axis=-1, eps=1e-05):
    m = jnp.mean(x, axis=axis, keepdims=True)
    v = jnp.var(x, axis=axis, keepdims=True)
    return (x - m) / jnp.sqrt(v + eps)

def _scatter_add(tgt, idx, src, axis=0):
    return tgt.at[idx].add(src)

def _segment_sum(src, seg, n):
    return jax.ops.segment_sum(src, seg, n)
kernel_name = 'mk_macaron_d2_jaxref_r8_595ff7'

def setup_inputs(seed: int=0):
    np.random.seed(seed)
    _w = jnp.asarray

    def _L0_attn_setup():
        import jax, jax.numpy as jnp
        import numpy as np
        EMBED_DIM = 128
        EXPAND_RATIO = 128
        B, N = (4, 256)

        def _rmsnorm(x, w, eps=1e-06):
            return x * jax.lax.rsqrt(jnp.mean(x * x, axis=-1, keepdims=True) + eps) * w

        def _gla_scan(q, k, v, g):
            b, n, h, d = q.shape
            qs, ks_, vs, gs = (jnp.moveaxis(t, 1, 0) for t in (q, k, v, g))
            S0 = jnp.zeros((b, h, d, d), dtype=q.dtype)

            def step(S, inp):
                q_t, k_t, v_t, g_t = inp
                S = jnp.exp(g_t)[..., :, None] * S + k_t[..., :, None] * v_t[..., None, :]
                o_t = jnp.einsum('bhk,bhkv->bhv', q_t, S)
                return (S, o_t)
            _, outs = jax.lax.scan(step, S0, (qs, ks_, vs, gs))
            return jnp.moveaxis(outs, 0, 1)
        key = jax.random.key(seed)
        ks = jax.random.split(key, 6)
        std = 0.02
        d = EMBED_DIM
        return {'x': jax.random.normal(ks[0], (B, N, d), dtype=jnp.float32), 'Wq': jax.random.normal(ks[1], (d, d), dtype=jnp.float32) * std, 'Wk': jax.random.normal(ks[2], (d, d), dtype=jnp.float32) * std, 'Wv': jax.random.normal(ks[3], (d, d), dtype=jnp.float32) * std, 'Wo': jax.random.normal(ks[4], (d, d), dtype=jnp.float32) * std, 'norm_w': jnp.ones((d,), dtype=jnp.float32)}
    _L0_attn_in = _L0_attn_setup()

    def _L0_ffn_setup():
        import jax, jax.numpy as jnp
        import numpy as np
        key = jax.random.key(seed)
        k0, k1, k2, k3 = jax.random.split(key, 4)
        B, S, D, F, E = (8, 256, 128, 256, 8)
        x = jax.random.normal(k0, (B, S, D), dtype=jnp.float32)
        Wg = jax.random.normal(k1, (D, E), dtype=jnp.float32) * 0.02
        W1 = jax.random.normal(k2, (E, D, F), dtype=jnp.float32) * 0.02
        W2 = jax.random.normal(k3, (E, F, D), dtype=jnp.float32) * 0.02
        return {'x': x, 'Wg': Wg, 'W1': W1, 'W2': W2}
    _L0_ffn_in = _L0_ffn_setup()

    def _L1_attn_setup():
        import jax, jax.numpy as jnp
        import numpy as np
        L, B, E = (256, 4, 128)
        S = 128
        EH = 2 * E
        CHUNK = 64
        MAXPOS = 64
        EPS = 1e-05

        def rope(x, axes):
            shape = x.shape
            spatial = [shape[i] for i in axes]
            total = int(np.prod(spatial))
            pos = jnp.arange(total, dtype=x.dtype).reshape(spatial)
            for _ in range(axes[-1] + 1, len(shape) - 1):
                pos = pos[..., None]
            half = shape[-1] // 2
            inv_freq = 10000.0 ** (-jnp.arange(half, dtype=x.dtype) / half)
            sinusoid = pos[..., None] * inv_freq
            sin, cos = (jnp.sin(sinusoid), jnp.cos(sinusoid))
            x1, x2 = jnp.split(x, 2, axis=-1)
            return jnp.concatenate([x1 * cos - x2 * sin, x2 * cos + x1 * sin], axis=-1)

        def rel_pos_bias(w, seq_len):
            t = jnp.pad(w[:2 * seq_len - 1], (0, seq_len))
            t = jnp.tile(t, seq_len)[:-seq_len].reshape(seq_len, 3 * seq_len - 2)
            r = (2 * seq_len - 1) // 2
            return t[:, r:-r]
        key = jax.random.key(seed)
        ks = jax.random.split(key, 12)

        def n(k, shape, std):
            return jax.random.normal(k, shape, dtype=jnp.float32) * std
        query = jax.random.normal(ks[0], (L, B, E), dtype=jnp.float32)
        return dict(query=query, key_in=query, value_in=query, ln_g=jnp.ones((E,), jnp.float32), ln_b=jnp.zeros((E,), jnp.float32), Wu=n(ks[1], (EH, E), 1.0 / np.sqrt(E)), bu=jnp.zeros((EH,), jnp.float32), Wv=n(ks[2], (EH, E), 1.0 / np.sqrt(E)), bv=jnp.zeros((EH,), jnp.float32), Wb=n(ks[3], (S, E), 1.0 / np.sqrt(E)), bb=jnp.zeros((S,), jnp.float32), qqw=n(ks[4], (S,), 0.02), qqb=jnp.zeros((S,), jnp.float32), qkw=n(ks[5], (S,), 0.02), qkb=jnp.zeros((S,), jnp.float32), lqw=n(ks[6], (S,), 0.02), lqb=jnp.zeros((S,), jnp.float32), lkw=n(ks[7], (S,), 0.02), lkb=jnp.zeros((S,), jnp.float32), Wo=n(ks[8], (E, EH), 1.0 / np.sqrt(EH)), bo=jnp.zeros((E,), jnp.float32), w_rel=n(ks[9], (2 * MAXPOS - 1,), 0.02))
    _L1_attn_in = _L1_attn_setup()

    def _L1_ffn_setup():
        import jax, jax.numpy as jnp
        import numpy as np
        E, D, MULT, K = (8, 128, 4, 2)
        B, S = (4, 256)
        H = MULT * D
        key = jax.random.key(seed)
        k0, k1, k2, k3 = jax.random.split(key, 4)
        x = jax.random.normal(k0, (B, S, D), dtype=jnp.float32)
        Wr = jax.random.normal(k1, (E, D), dtype=jnp.float32) * D ** (-0.5)
        W1 = jax.random.normal(k2, (E, D, H), dtype=jnp.float32) * D ** (-0.5)
        b1 = jnp.zeros((E, H), dtype=jnp.float32)
        W2 = jax.random.normal(k3, (E, H, D), dtype=jnp.float32) * H ** (-0.5)
        b2 = jnp.zeros((E, D), dtype=jnp.float32)
        return {'x': x, 'Wr': Wr, 'W1': W1, 'b1': b1, 'W2': W2, 'b2': b2}
    _L1_ffn_in = _L1_ffn_setup()
    _d = {'L0_attn_x': _L0_attn_in['x'], 'L0_attn_Wq': _L0_attn_in['Wq'], 'L0_attn_Wk': _L0_attn_in['Wk'], 'L0_attn_Wv': _L0_attn_in['Wv'], 'L0_attn_Wo': _L0_attn_in['Wo'], 'L0_attn_norm_w': _L0_attn_in['norm_w'], 'L0_ffn_Wg': _L0_ffn_in['Wg'], 'L0_ffn_W1': _L0_ffn_in['W1'], 'L0_ffn_W2': _L0_ffn_in['W2'], 'L1_attn_key_in': _L1_attn_in['key_in'], 'L1_attn_value_in': _L1_attn_in['value_in'], 'L1_attn_ln_g': _L1_attn_in['ln_g'], 'L1_attn_ln_b': _L1_attn_in['ln_b'], 'L1_attn_Wu': _L1_attn_in['Wu'], 'L1_attn_bu': _L1_attn_in['bu'], 'L1_attn_Wv': _L1_attn_in['Wv'], 'L1_attn_bv': _L1_attn_in['bv'], 'L1_attn_Wb': _L1_attn_in['Wb'], 'L1_attn_bb': _L1_attn_in['bb'], 'L1_attn_qqw': _L1_attn_in['qqw'], 'L1_attn_qqb': _L1_attn_in['qqb'], 'L1_attn_qkw': _L1_attn_in['qkw'], 'L1_attn_qkb': _L1_attn_in['qkb'], 'L1_attn_lqw': _L1_attn_in['lqw'], 'L1_attn_lqb': _L1_attn_in['lqb'], 'L1_attn_lkw': _L1_attn_in['lkw'], 'L1_attn_lkb': _L1_attn_in['lkb'], 'L1_attn_Wo': _L1_attn_in['Wo'], 'L1_attn_bo': _L1_attn_in['bo'], 'L1_attn_w_rel': _L1_attn_in['w_rel'], 'L1_ffn_Wr': _L1_ffn_in['Wr'], 'L1_ffn_W1': _L1_ffn_in['W1'], 'L1_ffn_b1': _L1_ffn_in['b1'], 'L1_ffn_W2': _L1_ffn_in['W2'], 'L1_ffn_b2': _L1_ffn_in['b2']}
    _x0 = _d['L0_attn_x']
    _d['L0_attn_x'] = jax.random.normal(jax.random.fold_in(jax.random.key(seed), 1), (4, 1024, 128), dtype=_x0.dtype)
    del _x0
    return _d

def reference(L0_attn_x, L0_attn_Wq, L0_attn_Wk, L0_attn_Wv, L0_attn_Wo, L0_attn_norm_w, L0_ffn_Wg, L0_ffn_W1, L0_ffn_W2, L1_attn_key_in, L1_attn_value_in, L1_attn_ln_g, L1_attn_ln_b, L1_attn_Wu, L1_attn_bu, L1_attn_Wv, L1_attn_bv, L1_attn_Wb, L1_attn_bb, L1_attn_qqw, L1_attn_qqb, L1_attn_qkw, L1_attn_qkb, L1_attn_lqw, L1_attn_lqb, L1_attn_lkw, L1_attn_lkb, L1_attn_Wo, L1_attn_bo, L1_attn_w_rel, L1_ffn_Wr, L1_ffn_W1, L1_ffn_b1, L1_ffn_W2, L1_ffn_b2):

    def _L0_attn_ref(x, Wq, Wk, Wv, Wo, norm_w):
        import jax, jax.numpy as jnp
        import numpy as np
        EMBED_DIM = 128
        EXPAND_RATIO = 128
        B, N = (4, 256)

        def _rmsnorm(x, w, eps=1e-06):
            return x * jax.lax.rsqrt(jnp.mean(x * x, axis=-1, keepdims=True) + eps) * w

        def _gla_scan(q, k, v, g):
            b, n, h, d = q.shape
            qs, ks_, vs, gs = (jnp.moveaxis(t, 1, 0) for t in (q, k, v, g))
            S0 = jnp.zeros((b, h, d, d), dtype=q.dtype)

            def step(S, inp):
                q_t, k_t, v_t, g_t = inp
                S = jnp.exp(g_t)[..., :, None] * S + k_t[..., :, None] * v_t[..., None, :]
                o_t = jnp.einsum('bhk,bhkv->bhv', q_t, S)
                return (S, o_t)
            _, outs = jax.lax.scan(step, S0, (qs, ks_, vs, gs))
            return jnp.moveaxis(outs, 0, 1)
        b, n, D = x.shape
        hd = EXPAND_RATIO
        h = D // hd
        q = jax.nn.silu(x @ Wq.T)
        f = jax.nn.sigmoid(x @ Wk.T)
        log_f = jax.nn.log_sigmoid(f)
        k = 1.0 - f
        v = x @ Wv.T

        def split_heads(t):
            return t.reshape(b, n, h, hd)
        out = _gla_scan(split_heads(q), split_heads(k), split_heads(v), split_heads(log_f))
        out = out.reshape(b, n, D)
        out = _rmsnorm(out, norm_w)
        return out @ Wo.T

    def _L0_ffn_ref(x, Wg, W1, W2):
        import jax, jax.numpy as jnp
        import numpy as np
        B, S, D = x.shape
        E = Wg.shape[1]
        T = B * S
        cap = max(1, T // E)
        xt = x.reshape(T, D)
        logits = xt @ Wg
        probs = jax.nn.softmax(logits, axis=-1)
        pT = probs.T
        _, top_idx = jax.lax.top_k(pT, cap)
        sel = jnp.zeros((E, T), dtype=bool).at[jnp.arange(E)[:, None], top_idx].set(True)
        masked = jnp.where(sel, pT, -jnp.inf)
        assigned = sel.any(axis=0)
        tok2exp = jnp.where(assigned, jnp.argmax(masked, axis=0), jnp.argmax(pT, axis=0))
        weights = jnp.take_along_axis(probs, tok2exp[:, None], axis=1)[:, 0]
        out = jnp.zeros_like(xt)
        for e in range(E):
            gate = jnp.where(tok2exp == e, weights, 0.0)
            h = jax.nn.gelu(xt @ W1[e], approximate=False) @ W2[e]
            out = out + gate[:, None] * h
        return out.reshape(B, S, D)

    def _L1_attn_ref(query, key_in, value_in, ln_g, ln_b, Wu, bu, Wv, bv, Wb, bb, qqw, qqb, qkw, qkb, lqw, lqb, lkw, lkb, Wo, bo, w_rel):
        import jax, jax.numpy as jnp
        import numpy as np
        L, B, E = (256, 4, 128)
        S = 128
        EH = 2 * E
        CHUNK = 64
        MAXPOS = 64
        EPS = 1e-05

        def rope(x, axes):
            shape = x.shape
            spatial = [shape[i] for i in axes]
            total = int(np.prod(spatial))
            pos = jnp.arange(total, dtype=x.dtype).reshape(spatial)
            for _ in range(axes[-1] + 1, len(shape) - 1):
                pos = pos[..., None]
            half = shape[-1] // 2
            inv_freq = 10000.0 ** (-jnp.arange(half, dtype=x.dtype) / half)
            sinusoid = pos[..., None] * inv_freq
            sin, cos = (jnp.sin(sinusoid), jnp.cos(sinusoid))
            x1, x2 = jnp.split(x, 2, axis=-1)
            return jnp.concatenate([x1 * cos - x2 * sin, x2 * cos + x1 * sin], axis=-1)

        def rel_pos_bias(w, seq_len):
            t = jnp.pad(w[:2 * seq_len - 1], (0, seq_len))
            t = jnp.tile(t, seq_len)[:-seq_len].reshape(seq_len, 3 * seq_len - 2)
            r = (2 * seq_len - 1) // 2
            return t[:, r:-r]
        tgt_len = query.shape[0]
        len_pad = (CHUNK - tgt_len % CHUNK) % CHUNK
        q = jnp.pad(query, ((0, len_pad), (0, 0), (0, 0)))
        Lp = q.shape[0]
        nc = Lp // CHUNK
        q = q.transpose(1, 0, 2)
        shortcut = q
        mu = q.mean(-1, keepdims=True)
        var = q.var(-1, keepdims=True)
        xn = (q - mu) / jnp.sqrt(var + EPS) * ln_g + ln_b
        u = jax.nn.silu(xn @ Wu.T + bu)
        v = jax.nn.silu(xn @ Wv.T + bv)
        base = jax.nn.silu(xn @ Wb.T + bb)
        bsz = q.shape[0]

        def mk(wt, bi):
            t = (base * wt + bi).reshape(bsz, nc, CHUNK, S)
            return rope(t, [1, 2])
        quad_q, quad_k = (mk(qqw, qqb), mk(qkw, qkb))
        lin_q, lin_k = (mk(lqw, lqb), mk(lkw, lkb))
        vch = v.reshape(bsz, nc, CHUNK, EH)
        quad_qk = jnp.einsum('bgne,bgme->bgnm', quad_q, quad_k)
        bias = rel_pos_bias(w_rel, MAXPOS)[:CHUNK, :CHUNK]
        kernel = jnp.square(jax.nn.relu(quad_qk / CHUNK + bias))
        causal = jnp.tril(jnp.ones((CHUNK, CHUNK), dtype=bool))
        kernel = jnp.where(causal, kernel, 0.0)
        quadratic = jnp.einsum('bgnm,bgme->bgne', kernel, vch)
        lin_kv = jnp.einsum('bgnk,bgne->bgke', lin_k, vch) / CHUNK
        cmask = jnp.tril(jnp.ones((nc, nc), dtype=lin_kv.dtype), k=-1)
        lin_kv = jnp.einsum('bhke,gh->bgke', lin_kv, cmask)
        linear = jnp.einsum('bgnk,bgke->bgne', lin_q, lin_kv)
        x = (u.reshape(bsz, nc, CHUNK, EH) * (linear + quadratic)).reshape(bsz, Lp, EH)
        x = x @ Wo.T + bo
        out = (x + shortcut).transpose(1, 0, 2)[:tgt_len]
        return out

    def _L1_ffn_ref(x, Wr, W1, b1, W2, b2):
        import jax, jax.numpy as jnp
        import numpy as np
        E, D, MULT, K = (8, 128, 4, 2)
        B, S = (4, 256)
        H = MULT * D
        probs = jax.nn.softmax(jnp.einsum('bsd,ed->bse', x, Wr), axis=-1)
        topv, topi = jax.lax.top_k(probs, K)
        combine = jnp.sum(topv[..., None] * jax.nn.one_hot(topi, E, dtype=x.dtype), axis=2)

        def body(acc, params):
            w1, bb1, w2, bb2, ce = params
            h = jax.nn.gelu(jnp.einsum('bsd,dh->bsh', x, w1) + bb1, approximate=False)
            y = jnp.einsum('bsh,hd->bsd', h, w2) + bb2
            return (acc + ce[..., None] * y, None)
        cE = jnp.moveaxis(combine, -1, 0)
        out, _ = jax.lax.scan(body, jnp.zeros_like(x), (W1, b1, W2, b2, cE))
        return out
    x = L0_attn_x
    x = x + 0.5 * _L0_ffn_ref(_layernorm(x, axis=-1), L0_ffn_Wg, L0_ffn_W1, L0_ffn_W2)
    x = x + _L0_attn_ref(_layernorm(x, axis=-1), L0_attn_Wq, L0_attn_Wk, L0_attn_Wv, L0_attn_Wo, L0_attn_norm_w)
    x = x + 0.5 * _L0_ffn_ref(_layernorm(x, axis=-1), L0_ffn_Wg, L0_ffn_W1, L0_ffn_W2)
    x = x + 0.5 * _L1_ffn_ref(_layernorm(x, axis=-1), L1_ffn_Wr, L1_ffn_W1, L1_ffn_b1, L1_ffn_W2, L1_ffn_b2)
    x = x + _L1_attn_ref(_layernorm(x, axis=-1), L1_attn_key_in, L1_attn_value_in, L1_attn_ln_g, L1_attn_ln_b, L1_attn_Wu, L1_attn_bu, L1_attn_Wv, L1_attn_bv, L1_attn_Wb, L1_attn_bb, L1_attn_qqw, L1_attn_qqb, L1_attn_qkw, L1_attn_qkb, L1_attn_lqw, L1_attn_lqb, L1_attn_lkw, L1_attn_lkb, L1_attn_Wo, L1_attn_bo, L1_attn_w_rel)
    x = x + 0.5 * _L1_ffn_ref(_layernorm(x, axis=-1), L1_ffn_Wr, L1_ffn_W1, L1_ffn_b1, L1_ffn_W2, L1_ffn_b2)
    return x

_drawn_inputs = setup_inputs


def setup_inputs(seed=0):
    import zlib

    import numpy as np

    out = dict(_drawn_inputs(seed))
    spreads = {'L0_attn_norm_w': (1.0, 0.2),
     'L1_attn_ln_g': (1.0, 0.6),
     'L1_attn_ln_b': (0.0, 0.8),
     'L1_attn_bu': (0.0, 0.8),
     'L1_attn_bv': (0.0, 0.8),
     'L1_attn_bb': (0.0, 0.8),
     'L1_attn_qqb': (0.0, 0.8),
     'L1_attn_qkb': (0.0, 0.8),
     'L1_attn_lqb': (0.0, 0.1),
     'L1_attn_lkb': (0.0, 0.1),
     'L1_attn_bo': (0.0, 0.1),
     'L1_ffn_b1': (0.0, 0.355),
     'L1_ffn_b2': (0.0, 0.1)}
    factors = {'L0_ffn_Wg': 6.192,
     'L0_ffn_W1': 6.326,
     'L0_ffn_W2': 6.092,
     'L1_attn_Wu': 8.0,
     'L1_attn_Wv': 8.0,
     'L1_attn_Wb': 8.0,
     'L1_attn_qqw': 8.0,
     'L1_attn_qkw': 8.0,
     'L1_attn_Wo': 8.0,
     'L1_attn_w_rel': 8.0}
    for name, (base, spread) in spreads.items():
        noise = np.random.default_rng([zlib.crc32(name.encode()), seed]).standard_normal(out[name].shape)
        drawn = base * np.exp(spread * noise) if base else spread * noise
        out[name] = jnp.asarray(drawn.astype(out[name].dtype))
    for name, factor in factors.items():
        out[name] = (out[name] * factor).astype(out[name].dtype)
    return out
```

```python
from contextlib import ExitStack

import concourse.bass as bass
from concourse import mybir

F32 = mybir.dt.float32
BF16 = mybir.dt.bfloat16
I32 = mybir.dt.int32
ALU = mybir.AluOpType
ACT = mybir.ActivationFunctionType
AX = mybir.AxisListType.X
ds = bass.ds

P = 128
E = 8
NMAX = 512

C_IDENT = 0
C_NEGMASK = 128
C_STRICT = 256
C_SAMEEXP = 384
C_RANK = 512
C_RESET = 520
C_END = 520 + 256


def program(nc, d, out):
    B, L, D = d["x"].shape
    T = B * L
    NT = T // P
    NS = T // NMAX
    TPS = NMAX // P
    F0 = d["w1_0"].shape[2]
    F1 = d["w1_1"].shape[2]
    FC0, FC1 = F0 // P, F1 // P
    CAP = T // E
    EH = d["wuT"].shape[1]
    assert D == P and NT * E == 256 and EH == 2 * P and B == 4

    ctx = ExitStack()
    with ctx:
        def sb(name, shape, dt=F32):
            return ctx.enter_context(nc.sbuf_tensor(name, shape, dt))

        def sem(name):
            return ctx.enter_context(nc.semaphore(name))

        def sems(stage, *names):
            return {n: sem(f"{stage}_{n}") for n in names}

        class Signals(dict):
            def at(self, name, count):
                return self[name], self.base[name] + count

        kinds = {}

        def layer_sems(kind, totals):
            have = kinds.setdefault(kind, {})
            s = Signals()
            s.base = {}
            for n, total in totals.items():
                if n not in have:
                    have[n] = [sem(f"{kind}_{n}"), 0]
                s[n], s.base[n] = have[n]
                have[n][1] += total
            return s

        bank = [ctx.enter_context(nc.psum_tensor(f"bank{i}", [P, NMAX], F32)) for i in range(8)]

        x = sb("x", [P, NT, P])
        RW = P + 2
        rows = sb("rows", [P, NT, RW])
        xn = rows[:, :, 0:P]
        turned = sb("turned", [P, 8192])
        xnT = turned[:, 0:4096]
        xh = turned[:, 4096:6144].bitcast(BF16)
        xl = turned[:, 6144:8192].bitcast(BF16)
        arena = sb("arena", [P, 11520])
        consts = sb("consts", [P, C_END])
        ident = consts[:, C_IDENT:C_IDENT + P]
        ident_bf = sb("ident_bf", [P, P], BF16)
        negmask = consts[:, C_NEGMASK:C_NEGMASK + P]
        same_expert = consts[:, C_SAMEEXP:C_SAMEEXP + P]
        rank_w = consts[:, C_RANK:C_RANK + E]
        reset = consts[:, C_RESET:C_RESET + NT * E]
        ones_bf = sb("ones_bf", [P, P], BF16)
        ones_f = sb("ones_f", [P, P])
        strict_bf = sb("strict_bf", [P, P], BF16)
        eps = sb("eps", [P, 16])
        credit = sb("credit", [P, 32])

        w1h0, w1l0 = (sb(f"w1{h}0", [P, E, F0], BF16) for h in "hl")
        w2h0, w2l0 = (sb(f"w2{h}0", [P, E, FC0, P], BF16) for h in "hl")
        w1h1, w1l1 = (sb(f"w1{h}1", [P, E, F1], BF16) for h in "hl")
        w2h1, w2l1 = (sb(f"w2{h}1", [P, E, FC1, P], BF16) for h in "hl")
        wr0 = sb("wr0", [P, E])
        wr1 = sb("wr1", [P, E])
        BR = 96
        BW = P + F1 + 2 * EH
        brows = sb("brows", [BR, BW], BF16)
        b2rows, b1rows, uvrows = brows[:, 0:P], brows[:, P:P + F1], brows[:, P + F1:BW]
        selector_i = sb("selector", [BR, E * F1], mybir.dt.uint16)
        selector = selector_i[:].bitcast(BF16)
        wqT, wkT, wvT, woT = (sb(n, [P, P]) for n in ("wqT_s", "wkT_s", "wvT_s", "woT_s"))
        wvh, wvl = sb("wvh", [P, P], BF16), sb("wvl", [P, P], BF16)
        normw = sb("normw", [P, 1])
        woTn = sb("woTn", [P, P])
        wuv = sb("wuv", [P, 2 * EH])
        wuvh, wuvl = sb("wuvh", [P, 2 * EH], BF16), sb("wuvl", [P, 2 * EH], BF16)
        wbT = sb("wbT_s", [P, P])
        wo1 = sb("wo1", [P, EH // P, P])
        cols = sb("cols", [P, 8])
        rot = sb("rot", [P, B, P])
        rotqk = sb("rotqk", [P, B, 2 * P])
        wrel = sb("wrel", [P, 4])
        bias10 = sb("bias10", [P, 10])
        bo_b = sb("bo_b", [P, P])

        stats = sb("stats", [P, NT, 6])
        mean = sb("mean", [P, NT])
        nwt = sb("nwt", [P, 8, NT])
        rt = sb("rt", [P, 12, NT * E])
        rotb = rt[0:1, 0:B, :]
        small = sb("small", [P, 6, NT])
        pT = rt[:, 10, :]
        pjunk = rt[:, 11, :]
        srch = sb("srch", [P, 24])
        thr_in = sb("thr_in", [E, 2, P])
        thr = sb("thr", [P, 2 * E])
        eqb = sb("eqb", [P, NT * E], BF16)
        W = 2 * P
        PAIRS = {1: T // W + E, 2: 2 * T // W + E}
        SLOT_TILES = {k: 2 * n for k, n in PAIRS.items()}
        CHUNK = 8
        CP = CHUNK // 2
        BODY = 2 * CP
        dest = sb("dest", [P, 2, NT], I32)
        slot_i = sb("slot_i", [P, 2, NT], I32)
        per_e = sb("per_e", [P, 6, E])
        per_ei = sb("per_ei", [P, 2, E], I32)
        starts = sb("starts", [1, 2, PAIRS[2]])
        tcmp = rt[0:1, 2:5, :].rearrange("p a b -> p (a b)")[:, 0:PAIRS[2] * E].rearrange("p (t e) -> p t e", e=E)
        tsum = rt[0:1, 0, 0:2 * PAIRS[2]].rearrange("p (a t) -> p a t", a=2)
        pair_e = sb("pair_e", [1, PAIRS[2] // BODY], I32)
        out_idx = sb("out_idx", [P, CHUNK], I32)
        pool_junk = sb("pool_junk", [P, 2 * PAIRS[1] + 2 * PAIRS[2]], BF16)

        block = ctx.enter_context(nc.Block())

        ld = sems("load", "consts", "x", "w0", "w1", "w1b", "consts2", "pad", "gla", "gau", "rows", "rows0")
        pr = sems("prep", "pool", "zero", "w0h", "w0l", "w1h", "w1l", "gla", "gau", "gau_mm", "rows")

        st_w1_0 = arena[:, 0:E * F0].rearrange("p (e f) -> p e f", e=E)
        st_w2_0 = arena[:, E * F0:2 * E * F0].rearrange("p (e c n) -> p e c n", e=E, c=FC0)
        o = SLOT_TILES[1] * (P + 2)
        st_w1_1 = arena[:, o:o + E * F1].rearrange("p (e f) -> p e f", e=E)
        st_w2_1 = arena[:, o:o + E * F1].rearrange("p (e c n) -> p e c n", e=E, c=FC1)

        x_tiles = lambda ap: ap.rearrange("b (a p) n -> p (b a) n", p=P)

        def load_sync(sp):
            sp.dma_start(x[:], x_tiles(d["x"])).then_inc(ld["x"], 16)
            sp.dma_start(consts[:], d["consts"]).then_inc(ld["consts"], 16)
            sp.dma_start(wr0[:], d["wg"]).then_inc(ld["consts"], 16)
            sp.dma_start(st_w1_0, d["w1_0"].rearrange("e k f -> k e f")).then_inc(ld["w0"], 16)
            sp.dma_start(dest[:], d["dest"]).then_inc(ld["consts2"], 16)
            sp.dma_start(starts[:], d["starts"]).then_inc(ld["consts2"], 16)
            sp.dma_start(selector_i[:], d["selector"]).then_inc(ld["consts2"], 16)
            sp.dma_start(slots["moe0"], d["pad1"]).then_inc(ld["pad"], 16)
            for t, n in ((wqT, "wqT"), (wkT, "wkT"), (wvT, "wvT"), (woT, "woT"), (normw, "norm_w")):
                sp.dma_start(t[:], d[n]).then_inc(ld["gla"], 16)
            sp.dma_start(st_w1_1, d["w1_1"].rearrange("e k f -> k e f")).then_inc(ld["w1"], 16)
            sp.dma_start(slots["moe2"], d["pad1"]).then_inc(ld["pad"], 16)
            sp.dma_start(slots["moe3"], d["pad2"]).then_inc(ld["pad"], 16)
            sp.dma_start(slots["moe6"], d["pad2"]).then_inc(ld["pad"], 16)
            sp.dma_start(wr1[:], d["wrT"]).then_inc(ld["w1"], 16)
            for t, n in ((wuv[:, 0:EH], "wvT1"), (wuv[:, EH:2 * EH], "wuT"), (wbT[:], "wbT"), (cols[:, 0:7], "cols"),
                         (rot[:], "rot"), (wo1[:], "wo1")):
                sp.dma_start(t, d[n]).then_inc(ld["gau"], 16)
            sp.dma_start(wrel[:], d["wrel"].partition_broadcast(P)).then_inc(ld["gau"], 16)
            sp.dma_start(bo_b[:], d["bo"].partition_broadcast(P)).then_inc(ld["gau"], 16)
            sp.wait_ge(pr["w1l"], 1)
            for e in range(E):
                sp.dma_start(st_w2_1[:, e], d["w2_1"][e].rearrange("(c p) n -> p c n", p=P)).then_inc(ld["w1b"], 16)

        def rows_pool(pool):
            flat = rt[0:BR].rearrange("p a b -> p (a b)")
            f = flat[:, 0:BW]
            a, b = (flat[:, o:o + BW // 2].bitcast(BF16) for o in (BW, BW + BW // 2))
            n = 0

            def done(ins):
                nonlocal n
                n += 1
                ins.then_inc(pr["rows"], 1)
                pool.wait_ge(pr["rows"], n)

            done(nc.gpsimd.memset(brows[:], 0.0))
            done(nc.gpsimd.memset(f, 0.0))
            for q in (0, 32, 64):
                pool.dma_start(f[q:q + E], d["brows"]).then_inc(ld["rows"], 16)
            pool.wait_ge(ld["rows"], 16 * 3)
            done(nc.gpsimd.tensor_copy(a, f))
            done(nc.gpsimd.tensor_tensor(f, f, a, ALU.subtract))
            done(nc.gpsimd.tensor_copy(b, f))
            done(nc.gpsimd.tensor_tensor(f, f, b, ALU.subtract))
            for q, part in ((0, a), (32, b), (64, f)):
                done(nc.gpsimd.tensor_copy(brows[q:q + E], part[q:q + E]))
        ROWS_DONE = 2 + 4 + 3

        LD_W0 = 16
        LD_W1 = 16 * 2
        LD_GAU = 16 * 8
        LD_GLA = 16 * 5

        def layernorm(stage, src, dst, source_ready, gb=None, halves=True):
            s = layer_sems("ln", dict(stat=NT, aggr=6, rsqrt=1 + RSQRT_STEPS, norm=NT, turned=NS,
                                      copied=NS * (2 if halves else 1), low=NS if halves else 0))
            s.update(src=src, dst=dst, ready=source_ready, gb=gb, halves=halves, copies=2 if halves else 1)
            return s

        def inverse_sqrt(dve, chain, n0, value, res):
            t, y, a, b = (nwt[:, i, :] for i in range(1, 5))
            n = n0

            def done(ins):
                nonlocal n
                n += 1
                ins.then_inc(chain, 1)
                dve.wait_ge(chain, n)

            done(nc.vector.tensor_scalar(t.bitcast(I32), value.bitcast(I32), 1, None, ALU.logical_shift_right))
            done(nc.vector.tensor_scalar(y.bitcast(I32), t.bitcast(I32), -1.0, float(0x5F3759DF), ALU.mult, ALU.add))
            for i in range(4):
                done(nc.vector.tensor_tensor(a, y, y, ALU.mult))
                done(nc.vector.scalar_tensor_tensor(b, a, -0.5, value, ALU.mult, ALU.mult))
                done(nc.vector.scalar_tensor_tensor(res if i == 3 else y, b, 1.5, y, ALU.add, ALU.mult))
            return n
        RSQRT_STEPS = 14

        def ln_vector(dve, s):
            src, dst = s["src"], s["dst"]
            for q, v in s["ready"]:
                dve.wait_ge(q, v)
            for t in range(NT):
                nc.vector.bn_stats(stats[:, t, :], src[:, t, :]).then_inc(s["stat"], 1)
            dve.wait_ge(*s.at("stat", NT))
            var, rs, sums, diff, msum = nwt[:, 0, :], nwt[:, 5, :], nwt[:, 6, :], nwt[:, 7, :], nwt[:, 1, :]
            me, mo = stats[:, :, 1], stats[:, :, 4]
            nc.vector.tensor_tensor(sums, me, mo, ALU.add).then_inc(s["aggr"], 1)
            nc.vector.tensor_tensor(diff, me, mo, ALU.subtract).then_inc(s["aggr"], 1)
            nc.vector.tensor_tensor(msum, stats[:, :, 2], stats[:, :, 5], ALU.add).then_inc(s["aggr"], 1)
            dve.wait_ge(*s.at("aggr", 3))
            nc.vector.tensor_scalar(mean[:], sums, 0.5, None, ALU.mult).then_inc(s["aggr"], 1)
            nc.vector.scalar_tensor_tensor(nwt[:, 2, :], diff, 0.25, diff, ALU.mult, ALU.mult).then_inc(s["aggr"], 1)
            nc.vector.tensor_scalar(nwt[:, 3, :], msum, 1.0 / P, 1e-5, ALU.mult, ALU.add).then_inc(s["aggr"], 1)
            dve.wait_ge(*s.at("aggr", 6))
            nc.vector.tensor_tensor(var, nwt[:, 2, :], nwt[:, 3, :], ALU.add).then_inc(s["rsqrt"], 1)
            dve.wait_ge(*s.at("rsqrt", 1))
            inverse_sqrt(dve, s["rsqrt"], s.base["rsqrt"] + 1, var, rs)
            for t in range(NT):
                nc.vector.tensor_scalar(dst[:, t, :], src[:, t, :], mean[:, t:t + 1], rs[:, t:t + 1],
                                        ALU.subtract, ALU.mult).then_inc(s["norm"], 1)
            if not s["halves"]:
                return
            for i in range(NS):
                dve.wait_ge(*s.at("copied", 2 * i + 2))
                o = slice(NMAX * i, NMAX * (i + 1))
                nc.vector.tensor_tensor(xl[:, o], xnT[:, o], xh[:, o], ALU.subtract).then_inc(s["low"], 1)

        def ln_tensor(pe, s):
            for i in range(NS):
                pe.wait_ge(*s.at("norm", TPS * (i + 1)))
                if i >= 2:
                    pe.wait_ge(*s.at("copied", s["copies"] * (i - 1)))
                for j in range(TPS):
                    last = nc.tensor.transpose(bank[i % 2][:, P * j:P * (j + 1)], s["dst"][:, TPS * i + j, :], ident)
                last.then_inc(s["turned"], 1)

        def ln_scalar(act, s):
            for i in range(NS):
                act.wait_ge(*s.at("turned", i + 1))
                for t in (xnT, xh)[0:s["copies"]]:
                    o = t[:, NMAX * i:NMAX * (i + 1)]
                    if s["gb"]:
                        ins = nc.scalar.activation(o, bank[i % 2][:], ACT.Identity, bias=s["gb"][1], scale=s["gb"][0])
                    else:
                        ins = nc.scalar.activation(o, bank[i % 2][:], ACT.Identity)
                    ins.then_inc(s["copied"], 1)

        warm_sem = sem("table_warm")
        warmed = [0]

        def warm(act, function):
            warmed[0] += 1
            c = warmed[0]
            nc.scalar.activation(eps[:, c:c + 1], eps[:, 0:1], function).then_inc(warm_sem, 1)

        G = E * NS
        R_LGT, R_P, R_GT, R_SEL, R_PM, R_TOT, R_INC, R_A, R_B, R_C, R_D, R_K1 = range(12)

        def v3(i):
            return rt[:, i, :].rearrange("p (t e) -> p t e", e=E)

        def over_e(a):
            return a.unsqueeze(2).to_broadcast([P, NT, E])

        def over_t(a):
            return a.unsqueeze(1).to_broadcast([P, NT, E])

        RINGS = dict(xT=2, act=2, low=2, down=4, y=2)
        RING = 2
        SEARCH = 15
        SK = 5

        scattered = [sem(f"scattered{k}") for k in range(CHUNK)]
        loaded_y = [sem(f"loaded_y{b}") for b in range(B)]
        SCATTERS = [1]
        YSB = SLOT_TILES[2] * RW
        slots, ydram = {}, {}
        for name, k in (("moe0", 1), ("moe2", 1), ("moe3", 2), ("moe6", 2)):
            n = SLOT_TILES[k]
            slots[name] = nc.dram_tensor(f"slots_{name}", [n * P, RW], F32, kind="Internal").ap()
            ydram[name] = nc.dram_tensor(f"y_{name}", [k * T + n * P, P], F32, kind="Internal").ap()
            SCATTERS.append(SCATTERS[-1] + n // CHUNK)

        def moe(stage, ln, index, FC, w1, w2, wr, bias, top2):
            K, n = (2 if top2 else 1), SLOT_TILES[2 if top2 else 1]
            s = layer_sems("moe", dict(logits=1, exp=1, ptT=2 - K, count=(2 - K) * (SEARCH + 1), thr=2 - K, prefix=3 - K,
                                       placed=3, cols=2 + (K - 1) * B, sent=16 * NT * K, rows=16 * (n // CHUNK),
                                       split=n // CHUNK, turned=n // 2, up=n // 2, comb=B,
                                       **{q: RINGS[q] + n // 2 for q in RINGS}))
            s["route"] = sem(f"{stage}_route")
            s.base["route"] = 0
            s.update(ln=ln, FC=FC, w1=w1, w2=w2, wr=wr, bias=bias, top2=top2, index=index)
            s["K"] = 2 if top2 else 1
            s["tiles"] = SLOT_TILES[s["K"]]
            s["before"] = SCATTERS[index]
            s["slots"], s["ydram"] = slots[stage], ydram[stage]
            s["pads"] = 16 * (index + 1)
            s["y_before"] = 16 * (0, 1, 2, 4)[index]
            s["in"] = arena[:, 0:s["tiles"] * RW].rearrange("p (t r) -> p t r", r=RW)
            s["pairs"] = s["tiles"] // 2
            s["ybuf"] = arena[:, 0:s["K"] * 4096].rearrange("p (k t n) -> p k t n", k=s["K"], n=P)
            o = 0

            def take(words):
                nonlocal o
                o += words
                return turned[:, o - words:o]
            s["xs"] = take(2 * CHUNK * P).bitcast(BF16).rearrange("p (h k t n) -> p h k t n", h=2, k=2, t=CHUNK)
            s["hh"], s["hl"] = (take(2 * FC * W).bitcast(BF16).rearrange("p (k n) -> p k n", k=4) for i in range(2))
            s["h32"] = take(2 * FC * W).rearrange("p (k n) -> p k n", k=2)
            s["xT_t"] = rt[:, 6:8, :].bitcast(BF16)
            s["ysb"] = arena[:, YSB:YSB + CHUNK * P].rearrange("p (k n) -> p k n", k=CHUNK)
            return s

        def moe_tensor(pe, s, weights=()):
            FC, ln = s["FC"], s["ln"]
            router = bank[6]
            pe.wait_ge(*ln.at("copied", ln["copies"] * NS))
            for t in range(NT):
                last = nc.tensor.matmul(router[:, E * t:E * t + E], xnT[:, P * t:P * t + P], s["wr"], start=True, stop=True)
            last.then_inc(s["logits"], 1)

            if not s["top2"]:
                pe.wait_ge(*s.at("route", 5))
                for k in range(2):
                    last = nc.tensor.transpose(bank[7][:, P * k:P * k + P], rt[:, R_P, P * k:P * k + P], ident)
                last.then_inc(s["ptT"], 1)
                for i in range(SEARCH):
                    pe.wait_ge(*s.at("route", ROUTE_SEARCH + SK * i + 2))
                    nc.tensor.matmul(bank[7][:, 256:259], same_expert, srch[:, 8:11], start=True, stop=True)\
                        .then_inc(s["count"], 1)
                end = ROUTE_SEARCH + SK * SEARCH
                pe.wait_ge(*s.at("route", end + 1))
                nc.tensor.matmul(bank[7][:, 256:257], same_expert, srch[:, 8:9], start=True, stop=True)\
                    .then_inc(s["count"], 1)
                pe.wait_ge(*s.at("route", end + 4))
                for k in range(2):
                    last = nc.tensor.transpose(bank[7][:, 260 + E * k:260 + E * k + E], thr_in[:, k, :], ident[0:E, 0:E])
                last.then_inc(s["thr"], 1)
                pe.wait_ge(*s.at("route", end + 7))
                nc.tensor.matmul(router[:, 0:256], strict_bf[:], eqb[:], start=True, stop=True)
                nc.tensor.matmul(router[:, 256:512], ones_bf[:, 0:P], eqb[:], start=True, stop=True).then_inc(s["prefix"], 1)
            pe.wait_ge(*s.at("placed", 1))
            nc.tensor.matmul(router[:, 0:256], strict_bf[:], eqb[:], start=True, stop=True)
            nc.tensor.matmul(router[:, 256:512], ones_bf[:, 0:P], eqb[:], start=True, stop=True).then_inc(s["prefix"], 1)

            (w1h, w1l), (w2h, w2l) = s["w1"], s["w2"]
            pairs = s["pairs"]
            pe.wait_ge(*s.at("placed", 3))
            for q, v in weights:
                pe.wait_ge(q, v)

            def packed(c):
                return pe.value_load(pair_e[0:1, ds(c, 1)], min_val=0, max_val=E ** BODY - 1)

            def expert(packs, k):
                return pe.snap((packs[k // BODY] // E ** (k % BODY)) % E * (FC * P))

            def turn(t, k):
                if k % CP == 0:
                    pe.wait_ge(*s.at("split", t // CP + 1))
                pe.wait_ge(*s.at("xT", t + 1))
                o = bank[7 * (k % 2)][:].bitcast(BF16)
                for h in range(2):
                    for j in range(2):
                        last = nc.tensor.transpose(o[:, W * h + P * j:W * h + P * j + P],
                                                   s["xs"][:, h, k // CP % 2, 2 * (k % CP) + j, :], ident_bf[:])
                last.then_inc(s["turned"], 1)

            def up(t, k, e):
                r = k % 2
                xT = s["xT_t"][:, r]
                pe.wait_ge(*s.at("xT", t + 1 + RING))
                pe.wait_ge(*s.at("act", t + 1))
                for u in range(FC):
                    o = bank[1 + 2 * r + u // 2][:, W * (u % 2):W * (u % 2) + W]
                    wh, wl = (w[:].rearrange("p e f -> p (e f)")[:, ds(e + P * u, P)] for w in (w1h, w1l))
                    if s["bias"]:
                        nc.tensor.matmul(o, b1rows[:, P * u:P * u + P], selector[:, ds(e, W)], start=True, stop=False)
                    nc.tensor.matmul(o, wh, xT[:, 0:W], start=not s["bias"], stop=False)
                    nc.tensor.matmul(o, wh, xT[:, W:2 * W], start=False, stop=False)
                    last = nc.tensor.matmul(o, wl, xT[:, 0:W], start=False, stop=True)
                last.then_inc(s["up"], 1)

            def down(t, k, e):
                r = k % 2
                y = [bank[5 + r][:, P * j:P * j + P] for j in range(2)]
                pe.wait_ge(*s.at("y", t + 1))
                pe.wait_ge(*s.at("low", t + 1 + RING))
                if s["bias"]:
                    for j in range(2):
                        nc.tensor.matmul(y[j], selector[:, ds(e, P)], b2rows, start=(j == 0), stop=False)
                for u in range(FC):
                    hh, hl = ([s[n][:, k % 4, W * u + P * j:W * u + P * j + P] for j in range(2)] for n in ("hh", "hl"))
                    wh, wl = (w[:].rearrange("p e c n -> p (e c n)")[:, ds(e + P * u, P)] for w in (w2h, w2l))
                    for j in range(2):
                        nc.tensor.matmul(y[j], hh[j], wh, start=(u + j == 0 and not s["bias"]), stop=False)
                        nc.tensor.matmul(y[j], hl[j], wh, start=False, stop=False)
                    for j in range(2):
                        last = nc.tensor.matmul(y[j], hh[j], wl, start=False, stop=(u == FC - 1 and j == 1))
                last.then_inc(s["down"], 1)

            turn(0, 0)
            turn(1, 1)
            packs = [packed(0)]
            up(0, 0, expert(packs, 0))
            turn(2, 2)
            up(1, 1, expert(packs, 1))
            with pe.Fori(0, pairs // BODY - 1) as c:
                packs = [packed(c), packed(c + 1)]
                e = [expert(packs, 0), expert(packs, 1)]
                for k in range(BODY):
                    t = BODY * c + k
                    turn(t + 3, k + 3)
                    e.append(expert(packs, k + 2))
                    up(t + 2, k + 2, e[k + 2])
                    down(t, k, e[k])
            packs = [packed(pairs // BODY - 1)]
            e = [expert(packs, k) for k in range(BODY)]
            for k in range(BODY):
                t = pairs - BODY + k
                if k + 3 < BODY:
                    turn(t + 3, k + 3)
                if k + 2 < BODY:
                    up(t + 2, k + 2, e[k + 2])
                down(t, k, e[k])

        def moe_scalar(act, s, meanwhile=lambda: None):
            FC = s["FC"]
            act.wait_ge(*s.at("route", 2))
            nc.scalar.activation(rt[:, R_A, :], rt[:, R_B, :], ACT.Exp).then_inc(s["exp"], 1)
            meanwhile()
            warm(act, ACT.Gelu)
            act.wait_ge(*s.at("placed", 3))
            with act.Fori(0, s["pairs"] // 4) as four:
                for k in range(4):
                    t, r = 4 * four + k, k % 2
                    act.wait_ge(*s.at("up", t + 1))
                    act.wait_ge(*s.at("low", t + 1))
                    act.wait_ge(*s.at("down", t + 1))
                    for i in range(FC // 2):
                        o = slice(NMAX * i, NMAX * (i + 1))
                        nc.scalar.activation(s["h32"][:, r, o], bank[1 + 2 * r + i][:], ACT.Gelu)
                        last = nc.scalar.activation(s["hh"][:, k, o], bank[1 + 2 * r + i][:], ACT.Gelu)
                    last.then_inc(s["act"], 1)

        ROUTE_SEARCH = 7

        def moe_vector(dve, s, meanwhile=lambda: None):
            FC, chain = s["FC"], s["route"]
            n = 0

            def done(ins):
                nonlocal n
                n += 1
                ins.then_inc(chain, 1)
                dve.wait_ge(chain, n)

            for q, ring in RINGS.items():
                nc.vector.memset(srch[:, 23:24], 0.0).then_inc(s[q], ring)
                dve.wait_ge(*s.at(q, ring))

            lg = bank[6][:, 0:256].rearrange("p (t e) -> p t e", e=E)
            p, p3 = rt[:, R_P, :], v3(R_P)
            dve.wait_ge(*s.at("logits", 1))
            done(nc.vector.tensor_reduce(small[:, 0, :], lg, AX, ALU.max))
            done(nc.vector.tensor_tensor(v3(R_B), lg, over_e(small[:, 0, :]), ALU.subtract))
            dve.wait_ge(*s.at("exp", 1))
            done(nc.vector.tensor_reduce(small[:, 1, :], v3(R_A), AX, ALU.add))
            done(nc.vector.reciprocal(small[:, 2, :], small[:, 1, :]))
            done(nc.vector.tensor_tensor(p3, v3(R_A), over_e(small[:, 2, :]), ALU.mult))

            def first_largest(value, maximum, onehot, sc_a, sc_b):
                done(nc.vector.tensor_reduce(maximum, v3(value), AX, ALU.max))
                done(nc.vector.tensor_tensor(v3(sc_a), v3(value), over_e(maximum), ALU.is_equal))
                done(nc.vector.tensor_tensor(v3(sc_b), v3(sc_a), over_t(rank_w), ALU.mult))
                done(nc.vector.tensor_reduce(small[:, 5, :], v3(sc_b), AX, ALU.max))
                done(nc.vector.tensor_tensor(v3(onehot), v3(sc_b), over_e(small[:, 5, :]), ALU.is_equal))

            def prefix_sums(ready):
                dve.wait_ge(*s.at("prefix", ready))
                tot = rt[:, R_TOT, :]
                done(nc.vector.tensor_copy(tot.rearrange("p (e t) -> p e t", e=E),
                                           bank[6][:, 256:512].rearrange("p (t e) -> p e t", e=E)))
                done(nc.vector.tensor_tensor_scan(rt[:, R_INC, :], reset, tot, 0.0, ALU.mult, ALU.add))
                done(nc.vector.tensor_tensor(rt[:, R_A, :], rt[:, R_INC, :], tot, ALU.subtract))
                done(nc.vector.tensor_tensor(v3(R_B), rt[:, R_A, :].rearrange("p (e t) -> p t e", e=E),
                                             bank[6][:, 0:256].rearrange("p (t e) -> p t e", e=E), ALU.add))

            if s["top2"]:
                first_largest(R_P, small[:, 3, :], R_K1, R_A, R_B)
                done(nc.vector.scalar_tensor_tensor(rt[:, R_C, :], rt[:, R_K1, :], -2.0, p, ALU.mult, ALU.add))
                first_largest(R_C, small[:, 4, :], R_D, R_A, R_B)
                done(nc.vector.tensor_tensor(eqb[:], rt[:, R_K1, :], rt[:, R_D, :], ALU.add))
                prefixes = 0
            else:
                i32 = lambda a: a.bitcast(I32)
                cand, T_, bits, cnt, kept, need = (srch[:, a:b] for a, b in
                                                   ((0, 3), (3, 4), (4, 7), (8, 11), (12, 16), (16, 17)))
                done(nc.vector.memset(i32(T_), 0))
                for k in range(3):
                    last = nc.vector.memset(i32(bits[:, k:k + 1]), (k + 1) << 28)
                done(last)
                assert n == ROUTE_SEARCH
                dve.wait_ge(*s.at("ptT", 1))
                nc.vector.tensor_copy(pT, bank[7][:, 0:256]).then_inc(s["cols"], 1)
                dve.wait_ge(*s.at("cols", 1))
                for i in range(SEARCH):
                    base = i * SK + ROUTE_SEARCH
                    nc.vector.tensor_tensor(i32(cand), i32(T_).to_broadcast([P, 3]), i32(bits), ALU.bitwise_or)\
                        .then_inc(chain, 1)
                    dve.wait_ge(chain, base + 1)
                    for k in range(3):
                        last = nc.vector.tensor_scalar(rt[:, 7 + k, :] if k else pjunk, pT, cand[:, k:k + 1], None,
                                                       ALU.is_ge, ALU.add, accum_out=cnt[:, k:k + 1])
                    last.then_inc(chain, 1)
                    nc.vector.tensor_scalar(i32(bits), i32(bits), 2, None, ALU.logical_shift_right).then_inc(chain, 1)
                    nc.vector.tensor_copy(kept[:, 3:4], T_)
                    dve.wait_ge(*s.at("count", i + 1))
                    nc.vector.scalar_tensor_tensor(kept[:, 0:3], bank[7][:, 256:259], CAP - 0.5, cand,
                                                   ALU.is_ge, ALU.mult).then_inc(chain, 1)
                    dve.wait_ge(chain, base + 4)
                    nc.vector.tensor_reduce(T_, kept, AX, ALU.max).then_inc(chain, 1)
                    dve.wait_ge(chain, base + 5)
                n += SK * SEARCH
                done(nc.vector.tensor_scalar(pjunk, pT, T_, None, ALU.is_gt, ALU.add, accum_out=cnt[:, 0:1]))
                dve.wait_ge(*s.at("count", SEARCH + 1))
                done(nc.vector.tensor_scalar(need, bank[7][:, 256:257], -1.0, float(CAP), ALU.mult, ALU.add))
                done(nc.vector.tensor_copy(thr_in[:, 0, :], T_[0:E].to_broadcast([E, P])))
                done(nc.vector.tensor_copy(thr_in[:, 1, :], need[0:E].to_broadcast([E, P])))
                dve.wait_ge(*s.at("thr", 1))
                done(nc.vector.tensor_copy(thr[:], bank[7][:, 260:260 + 2 * E]))
                done(nc.vector.tensor_tensor(v3(R_GT), p3, over_t(thr[:, 0:E]), ALU.is_gt))
                done(nc.vector.tensor_tensor(eqb[:].rearrange("p (t e) -> p t e", e=E), p3, over_t(thr[:, 0:E]),
                                             ALU.is_equal))
                prefix_sums(1)
                done(nc.vector.tensor_tensor(v3(R_C), v3(R_B), over_t(thr[:, E:2 * E]), ALU.is_lt))
                done(nc.vector.tensor_tensor(rt[:, R_D, :], rt[:, R_C, :], eqb[:], ALU.mult))
                done(nc.vector.tensor_tensor(rt[:, R_SEL, :], rt[:, R_D, :], rt[:, R_GT, :], ALU.add))
                done(nc.vector.tensor_tensor(rt[:, R_A, :], rt[:, R_SEL, :], p, ALU.mult))
                done(nc.vector.scalar_tensor_tensor(rt[:, R_PM, :], rt[:, R_SEL, :], 1.0, rt[:, R_A, :],
                                                    ALU.subtract, ALU.add))
                done(nc.vector.tensor_reduce(small[:, 3, :], v3(R_SEL), AX, ALU.max))
                done(nc.vector.tensor_scalar(small[:, 4, :], small[:, 3, :], -1.0, 1.0, ALU.mult, ALU.add))
                done(nc.vector.tensor_tensor(v3(R_B), p3, over_e(small[:, 4, :]), ALU.mult))
                done(nc.vector.tensor_tensor(v3(R_C), v3(R_B), over_e(small[:, 3, :]), ALU.subtract))
                done(nc.vector.tensor_tensor(rt[:, R_D, :], rt[:, R_C, :], rt[:, R_PM, :], ALU.max))
                first_largest(R_D, small[:, 4, :], R_K1, R_A, R_B)
                done(nc.vector.tensor_copy(eqb[:], rt[:, R_K1, :]))
                prefixes = 1

            nc.vector.memset(srch[:, 23:24], 0.0).then_inc(s["placed"], 1)
            prefix_sums(prefixes + 1)
            padded, first, end, slot_end = (per_e[:, i, :] for i in range(4))
            total = rt[:, R_INC, :].rearrange("p (e t) -> p e t", e=E)[:, :, NT - 1]
            bits_w = W.bit_length() - 1
            done(nc.vector.tensor_scalar(per_ei[:, 0, :], total, float(W - 1), None, ALU.add))
            done(nc.vector.tensor_scalar(per_ei[:, 1, :], per_ei[:, 0, :], bits_w, bits_w, ALU.logical_shift_right,
                                         ALU.logical_shift_left))
            done(nc.vector.tensor_copy(padded, per_ei[:, 1, :]))
            done(nc.vector.tensor_tensor_scan(end, ones_f[:, 0:E], padded, 0.0, ALU.mult, ALU.add))
            done(nc.vector.tensor_tensor(first, end, padded, ALU.subtract))
            done(nc.vector.tensor_tensor(v3(R_C), v3(R_B), over_t(first), ALU.add))
            for k, onehot in ((0, R_K1), (1, R_D))[0:s["K"]]:
                done(nc.vector.tensor_tensor(rt[:, R_A, :], rt[:, R_C, :], rt[:, onehot, :], ALU.mult))
                done(nc.vector.tensor_reduce(small[:, 1 + k, :], v3(R_A), AX, ALU.add))
                done(nc.vector.tensor_copy(slot_i[:, k, :], small[:, 1 + k, :]))
                done(nc.vector.scalar_tensor_tensor(rt[:, R_B, :], p, 0.5, rt[:, onehot, :], ALU.mult, ALU.mult))
                done(nc.vector.tensor_reduce(small[:, 3 + k, :], v3(R_B), AX, ALU.add))
            gates = [small[:, 3, :], small[:, 4, :]]

            def columns(k):
                nc.vector.tensor_copy(rows[:, :, P].bitcast(I32), dest[:, k, :])
                nc.vector.tensor_copy(rows[:, :, P + 1], gates[k]).then_inc(s["cols"], 1)

            dve.wait_ge(ld["consts2"], 48)
            columns(0)
            pairs = s["pairs"]
            done(nc.vector.tensor_tensor(tcmp[:, 0:pairs], starts[:, 0, 0:pairs].unsqueeze(2).to_broadcast([1, pairs, E]),
                                         end[0:1].unsqueeze(1).to_broadcast([1, pairs, E]), ALU.is_ge))
            done(nc.vector.tensor_reduce(tsum[:, 0, 0:pairs], tcmp[:, 0:pairs], AX, ALU.add))
            done(nc.vector.tensor_scalar(tsum[:, 1, 0:pairs], tsum[:, 0, 0:pairs], float(E - 1), None, ALU.min))
            done(nc.vector.tensor_tensor(tsum[:, 0, 0:pairs], tsum[:, 1, 0:pairs], starts[:, 1, 0:pairs], ALU.mult))
            done(nc.vector.tensor_reduce(tsum[:, 1, 0:pairs // BODY],
                                         tsum[:, 0, 0:pairs].rearrange("p (c k) -> p c k", k=BODY), AX, ALU.add))
            nc.vector.tensor_copy(pair_e[:, 0:pairs // BODY], tsum[:, 1, 0:pairs // BODY]).then_inc(s["placed"], 2)
            if s["K"] == 2:
                dve.wait_ge(*s.at("sent", 16 * NT))
                columns(1)

            def split(c):
                dve.wait_ge(*s.at("rows", 16 * c + 16))
                src = s["in"][:, ds(CHUNK * c, CHUNK), 0:P]
                h, l = (s["xs"][:, i, ds(c % 2, 1)].squeeze(1) for i in range(2))
                nc.vector.tensor_copy(h, src).then_inc(chain, 1)
                dve.wait_ge(chain, c + (n + 1))
                nc.vector.tensor_tensor(l, src, h, ALU.subtract).then_inc(s["split"], 1)

            def copy_turned(t, k):
                dve.wait_ge(*s.at("turned", t + 1))
                if k >= 2:
                    dve.wait_ge(*s.at("up", t - 1))
                nc.vector.tensor_copy(s["xT_t"][:, k % 2], bank[7 * (k % 2)][:].bitcast(BF16)[:, 0:2 * W])\
                    .then_inc(s["xT"], 1)

            def low(t, k):
                r = k % 2
                dve.wait_ge(*s.at("act", t + 1 + RING))
                nc.vector.tensor_tensor(s["hl"][:, k % 4], s["h32"][:, r], s["hh"][:, k % 4], ALU.subtract)\
                    .then_inc(s["low"], 1)

            def finish(t, k):
                dve.wait_ge(*s.at("down", t + 1 + RINGS["down"]))
                for j in range(2):
                    slot, tile = 2 * (k % CP) + j, 2 * t + j
                    dve.wait_ge(scattered[slot], 16 * (s["before"] + t // CP))
                    nc.vector.tensor_copy(out_idx[:, slot:slot + 1], s["in"][:, ds(tile, 1), P].bitcast(I32))
                    last = nc.vector.tensor_scalar(s["ysb"][:, slot], bank[5 + k % 2][:, P * j:P * j + P],
                                                   s["in"][:, ds(tile, 1), P + 1], None, ALU.mult)
                last.then_inc(s["y"], 1)

            meanwhile()
            split(0)
            copy_turned(0, 0)
            copy_turned(1, 1)
            low(0, 0)
            copy_turned(2, 2)
            with dve.Fori(0, pairs // BODY - 1) as c:
                for k in range(BODY):
                    t = BODY * c + k
                    if k % CP == 0:
                        split(2 * c + k // CP + 1)
                    copy_turned(t + 3, k + 3)
                    low(t + 1, k + 1)
                    finish(t, k)
            for k in range(BODY):
                t = pairs - BODY + k
                if k == 0:
                    split(pairs // CP - 1)
                if k + 3 < BODY:
                    copy_turned(t + 3, k + 3)
                if k + 1 < BODY:
                    low(t + 1, k + 1)
                finish(t, k)

            for b in range(B):
                tb = slice(NT // B * b, NT // B * (b + 1))
                for k in range(s["K"]):
                    dve.wait_ge(loaded_y[b], s["y_before"] + 16 * s["K"])
                    ins = nc.vector.tensor_tensor(x[:, tb], x[:, tb], s["ybuf"][:, k, tb], ALU.add)
                    if k < s["K"] - 1:
                        ins.then_inc(s["cols"], 1)
                        dve.wait_ge(*s.at("cols", 2 + b + 1))
                ins.then_inc(s["comb"], 1)

        def moe_sync(sp, s, place_free=()):
            sp.wait_ge(*s.at("sent", 16 * NT * s["K"]))
            for q, v in place_free:
                sp.wait_ge(q, v)
            for c in range(s["tiles"] // CHUNK):
                sp.dma_start(s["in"][:, CHUNK * c:CHUNK * (c + 1), :],
                             s["slots"].rearrange("(t p) r -> p t r", p=P)[:, CHUNK * c:CHUNK * (c + 1), :])\
                    .then_inc(s["rows"], 16)
                sp.wait_ge(*s.at("rows", 16 * c + 16))
            for k in range(CHUNK):
                sp.wait_ge(scattered[k], 16 * (s["before"] + s["tiles"] // CHUNK))
            for b in range(B):
                tb = slice(NT // B * b, NT // B * (b + 1))
                for k in range(s["K"]):
                    y = s["ydram"][T * k:T * (k + 1)].rearrange("(t p) n -> p t n", p=P)
                    sp.dma_start(s["ybuf"][:, k, tb], y[:, tb]).then_inc(loaded_y[b], 16)

        def moe_pool(pool, s):
            pool.wait_ge(ld["pad"], s["pads"])
            cols = 1 if s["top2"] else 2
            for k in range(s["K"]):
                pool.wait_ge(*s.at("cols", cols + k))
                for t in range(NT):
                    nc.gpsimd.indirect_dma_start(
                        out=s["slots"], out_offset=bass.IndirectOffsetOnAxis(ap=slot_i[:, k, t:t + 1], axis=0),
                        in_=rows[:, t, :], in_offset=None).then_inc(s["sent"], 16)
            with pool.Fori(0, s["tiles"] // CHUNK) as c:
                for k in range(CHUNK):
                    t = CHUNK * c + k
                    if k % 2 == 0:
                        pool.wait_ge(*s.at("y", CP * c + k // 2 + 1 + RING))
                        nc.gpsimd.tensor_copy(pool_junk[:, ds(CP * c + k // 2 + CP * (s["before"] - 1), 1)], ones_bf[:, 0:1])
                    nc.gpsimd.indirect_dma_start(
                        out=s["ydram"], out_offset=bass.IndirectOffsetOnAxis(ap=out_idx[:, k:k + 1], axis=0),
                        in_=s["ysb"][:, k], in_offset=None).then_inc(scattered[k], 16)

        CH = NT // B
        HALF = P // 2

        gl = sems("gla", "q", "qcopied", "f", "fused", "a", "dve", "scaled", "st1", "act1", "am", "st2",
                  "state", "act2", "y", "ycopied", "rs", "add")
        ga = {}
        ga["qT"] = arena[:, 0:4096]
        ga["f"] = arena[:, 4096:5120].rearrange("p (k n) -> p k n", k=2)
        ga["a"] = arena[:, 5120:6144].rearrange("p (k n) -> p k n", k=2)
        ga["c"] = arena[:, 6144:7168].rearrange("p (k n) -> p k n", k=2)
        ga["r"] = arena[:, 7168:8192].rearrange("p (k n) -> p k n", k=2)
        ga["k"] = arena[:, 8192:9216].rearrange("p (k n) -> p k n", k=2)
        for i, n in enumerate(("kt", "v", "am", "oT", "sq", "S", "tmp")):
            o = 9216 + 256 * i
            ga[n] = arena[:, o:o + 256].rearrange("p (k n) -> p k n", k=2)
        ga["zero"] = arena[:, 11008:11136]
        ga["ss"] = sb("gla_ss", [P, NT])
        gy = xn

        def gla_tensor(pe, ln):
            pe.wait_ge(*ln.at("copied", 2 * NS))
            pe.wait_ge(*ln.at("low", NS))
            pe.wait_ge(pr["gla"], 4)
            with pe.Fori(0, NS // 2) as half:
                i = 2 * half
                for k in range(2):
                    pe.wait_ge(gl["qcopied"], i + k + 1)
                    nc.tensor.matmul(bank[k][:], wqT[:], xnT[:, ds(NMAX * (i + k), NMAX)], start=True, stop=True)\
                        .then_inc(gl["q"], 1)
            A, KV, O, DS, Y, FB = (bank[0], bank[1]), (bank[2], bank[3]), bank[4], bank[5], bank[6], bank[7]
            pe.wait_ge(gl["qcopied"], NS + 2)
            with pe.Fori(0, B) as b:
                for k in range(2):
                    pe.wait_ge(gl["fused"], 2 * b + k + 1)
                    nc.tensor.matmul(FB[:], wkT[:], xnT[:, ds(2 * NMAX * b + NMAX * k, NMAX)], start=True, stop=True)\
                        .then_inc(gl["f"], 1)

                def stage1(i):
                    n, k, c = CH * b + i, i // TPS, slice(P * (i % TPS), P * (i % TPS) + P)
                    tok = ds(2 * NMAX * b + P * i, P)
                    kv = KV[i % 2]
                    pe.wait_ge(gl["act1"], n + 1)
                    nc.tensor.matmul(kv[:, P:2 * P], xh[:, tok], wvh[:], start=True, stop=False)
                    nc.tensor.matmul(kv[:, P:2 * P], xl[:, tok], wvh[:], start=False, stop=False)
                    nc.tensor.matmul(kv[:, P:2 * P], xh[:, tok], wvl[:], start=False, stop=True)
                    pe.wait_ge(gl["scaled"], 2 * b + k + 3)
                    nc.tensor.transpose(kv[:, 0:P], ga["k"][:, k, c], ident)
                    pe.wait_ge(gl["am"], n + 1)
                    nc.tensor.matmul(A[i % 2][:, 0:P], ga["k"][:, k, c], ga["qT"][:, tok], start=True, stop=True)\
                        .then_inc(gl["st1"], 1)

                def stage2(i):
                    n = CH * b + i
                    tok = ds(2 * NMAX * b + P * i, P)
                    pe.wait_ge(gl["act1"], n + 3)
                    pe.wait_ge(gl["state"], n + 1)
                    nc.tensor.matmul(DS[:, 0:P], ga["kt"][:, i % 2], ga["v"][:, i % 2], start=True, stop=True)
                    pe.wait_ge(gl["am"], n + 3)
                    pe.wait_ge(gl["act2"], n + 1)
                    nc.tensor.matmul(O[:, 0:P], ga["v"][:, i % 2], ga["am"][:, i % 2], start=True, stop=False)
                    state = ga["S"][:, i % 2] if i > 0 else ga["zero"]
                    nc.tensor.matmul(O[:, 0:P], state, ga["qT"][:, tok], start=False, stop=True).then_inc(gl["st2"], 1)

                def stage3(i):
                    n = CH * b + i
                    pe.wait_ge(gl["act2"], n + 2)
                    pe.wait_ge(gl["ycopied"], n + 1)
                    nc.tensor.matmul(Y[:, 0:P], ga["oT"][:, i % 2], woTn[:], start=True, stop=True)
                    nc.tensor.matmul(Y[:, P:P + 1], ga["sq"][:, i % 2], ones_f[:, 0:1], start=True, stop=True)\
                        .then_inc(gl["y"], 1)

                for i in range(CH + 2):
                    if i < CH:
                        stage1(i)
                    if 1 <= i <= CH:
                        stage2(i - 1)
                    if i >= 2:
                        stage3(i - 2)

        def gla_scalar(act, ln):
            warm(act, ACT.Silu)
            with act.Fori(0, NS // 2) as half:
                i = 2 * half
                for k in range(2):
                    act.wait_ge(gl["q"], i + k + 1)
                    nc.scalar.activation(ga["qT"][:, ds(NMAX * (i + k), NMAX)], bank[k][:], ACT.Silu)\
                        .then_inc(gl["qcopied"], 1)
            warm(act, ACT.Sigmoid)
            with act.Fori(0, B) as b:
                def decay(k):
                    act.wait_ge(gl["f"], 2 * b + k + 1)
                    act.wait_ge(gl["scaled"], 2 * b + k + 1)
                    nc.scalar.activation(ga["f"][:, k], bank[7][:], ACT.Sigmoid).then_inc(gl["fused"], 1)
                    act.wait_ge(gl["fused"], 2 * b + k + 2)
                    nc.scalar.activation(ga["a"][:, k], ga["f"][:, k], ACT.Sigmoid).then_inc(gl["a"], 1)

                def copy1(i):
                    n = CH * b + i
                    act.wait_ge(gl["st1"], n + 1)
                    act.wait_ge(gl["st2"], n + 1)
                    nc.scalar.activation(ga["kt"][:, i % 2], bank[2 + i % 2][:, 0:P], ACT.Copy)
                    nc.scalar.activation(ga["v"][:, i % 2], bank[2 + i % 2][:, P:2 * P], ACT.Copy)\
                        .then_inc(gl["act1"], 1)

                def copy2(i):
                    n = CH * b + i
                    act.wait_ge(gl["st2"], n + 3)
                    act.wait_ge(gl["y"], n + 1)
                    nc.scalar.activation(ga["oT"][:, i % 2], bank[4][:, 0:P], ACT.Copy)
                    nc.scalar.activation(ga["sq"][:, i % 2], bank[4][:, 0:P], ACT.Square).then_inc(gl["act2"], 1)

                def copy3(i):
                    n = CH * b + i
                    act.wait_ge(gl["y"], n + 3)
                    nc.scalar.activation(gy[:, ds(n, 1), :], bank[6][:, 0:P].unsqueeze(1), ACT.Copy)
                    nc.scalar.activation(ga["ss"][:, ds(n, 1)], bank[6][:, P:P + 1], ACT.Copy)\
                        .then_inc(gl["ycopied"], 1)

                decay(0)
                decay(1)
                for i in range(CH + 2):
                    if i < CH:
                        copy1(i)
                    if 1 <= i <= CH:
                        copy2(i - 1)
                    if i >= 2:
                        copy3(i - 2)

        def gla_vector(dve, ln):
            for i, (q, v) in enumerate((("qcopied", 2), ("fused", 1), ("scaled", 2), ("act1", 2), ("am", 2), ("state", 1),
                                        ("act2", 1), ("st2", 2), ("y", 2), ("ycopied", 1))):
                nc.vector.memset(credit[:, i:i + 1], 0.0).then_inc(gl[q], v)
            c, r, f, a, kn = (ga[n] for n in ("c", "r", "f", "a", "k"))
            for ap in (ga["zero"], ga["am"]):
                last = nc.vector.memset(ap, 0.0)
            last.then_inc(pr["gla"], 1)
            dve.wait_ge(ld["gla"], LD_GLA)
            nc.vector.tensor_copy(wvh[:], wvT[:]).then_inc(pr["gla"], 1)
            dve.wait_ge(pr["gla"], 2)
            nc.vector.tensor_tensor(wvl[:], wvT[:], wvh[:], ALU.subtract).then_inc(pr["gla"], 1)
            nc.vector.tensor_scalar(woTn[:], woT[:], normw[:, 0:1], None, ALU.mult).then_inc(pr["gla"], 1)
            CHAIN = 8 + CH

            with dve.Fori(0, B) as b:
                def setup(k):
                    at = b * CHAIN + 4 * k
                    dve.wait_ge(gl["a"], 2 * b + k + 1)
                    dve.wait_ge(gl["state"], CH * b + 1)
                    for h in range(NMAX // HALF):
                        seg = slice(HALF * h, HALF * h + HALF)
                        last = nc.vector.tensor_tensor_scan(c[:, k, seg], a[:, k, seg], ga["zero"][:, 0:HALF], 1.0,
                                                            ALU.mult, ALU.add)
                    last.then_inc(gl["dve"], 1)
                    dve.wait_ge(gl["dve"], at + 1)
                    nc.vector.reciprocal(r[:, k], c[:, k]).then_inc(gl["dve"], 1)
                    q = ga["qT"][:, ds(2 * NMAX * b + NMAX * k, NMAX)]
                    nc.vector.tensor_tensor(q, q, c[:, k], ALU.mult).then_inc(gl["dve"], 1)
                    dve.wait_ge(gl["dve"], at + 3)
                    nc.vector.scalar_tensor_tensor(kn[:, k], f[:, k], 1.0, r[:, k], ALU.subtract, ALU.mult)\
                        .then_inc(gl["dve"], 1)
                    dve.wait_ge(gl["dve"], at + 4)
                    for j in range(TPS):
                        mid = slice(P * j + HALF - 1, P * j + HALF)
                        q1 = ga["qT"][:, ds(2 * NMAX * b + NMAX * k + P * j, HALF)]
                        k1 = kn[:, k, P * j:P * j + HALF]
                        nc.vector.tensor_scalar(q1, q1, r[:, k, mid], None, ALU.mult)
                        last = nc.vector.tensor_scalar(k1, k1, c[:, k, mid], None, ALU.mult)
                    last.then_inc(gl["scaled"], 1)

                def mask(i):
                    n = CH * b + i
                    A, am = bank[i % 2], ga["am"][:, i % 2]
                    dve.wait_ge(gl["st1"], n + 1)
                    dve.wait_ge(gl["st2"], n + 1)
                    nc.vector.tensor_tensor(am[0:HALF], A[0:HALF, 0:P], negmask[0:HALF], ALU.mult)
                    nc.vector.tensor_tensor(am[HALF:P, HALF:P], A[HALF:P, HALF:P], negmask[HALF:P, HALF:P],
                                            ALU.mult).then_inc(gl["am"], 1)

                def state(i):
                    n, at = CH * b + i, b * CHAIN + 8 + i
                    e2 = c[:, i // TPS, P * (i % TPS) + P - 1:P * (i % TPS) + P]
                    nx = min(i + 1, CH - 1)
                    e1 = c[:, nx // TPS, P * (nx % TPS) + HALF - 1:P * (nx % TPS) + HALF]
                    cur = ga["S"][:, i % 2] if i > 0 else ga["zero"]
                    dve.wait_ge(gl["st2"], n + 3)
                    dve.wait_ge(gl["state"], n + 1)
                    nc.vector.tensor_tensor(ga["tmp"][:, i % 2], cur, bank[5][:, 0:P], ALU.subtract).then_inc(gl["dve"], 1)
                    dve.wait_ge(gl["dve"], at + 1)
                    nc.vector.tensor_scalar(ga["S"][:, (i + 1) % 2], ga["tmp"][:, i % 2], e2, e1, ALU.mult, ALU.mult)\
                        .then_inc(gl["state"], 1)

                setup(0)
                setup(1)
                for i in range(CH + 1):
                    if i < CH:
                        mask(i)
                    if i >= 1:
                        state(i - 1)
            ms, rs = nwt[:, 0, :], nwt[:, 5, :]
            dve.wait_ge(gl["ycopied"], NT + 1)
            nc.vector.tensor_scalar(ms, ga["ss"][:], 1.0 / P, 1e-6, ALU.mult, ALU.add).then_inc(gl["rs"], 1)
            dve.wait_ge(gl["rs"], 1)
            inverse_sqrt(dve, gl["rs"], 1, ms, rs)
            with dve.Fori(0, NT) as t:
                xt = x[:, ds(t, 1), :]
                nc.vector.scalar_tensor_tensor(xt, gy[:, ds(t, 1), :], rs[:, ds(t, 1)], xt, ALU.mult, ALU.add)\
                    .then_inc(gl["add"], 1)

        NJ = L // P
        au = sems("gau", "b", "bs", "uvp", "uv", "qkp", "qkc", "dve", "z", "zt", "ztc", "o", "add", "rb")
        uv = arena[:, 0:4096].rearrange("p (k n f) -> p k n f", k=2, n=B)
        qk = arena[:, 4096:6144].rearrange("p (k n f) -> p k n f", k=2, n=B)
        bs = arena[:, 6144:7168].rearrange("p (k f) -> p k f", k=2)
        z = arena[:, 7168:9216].rearrange("p (k n f) -> p k n f", k=2, n=B)
        zT = arena[:, 9216:10240].rearrange("p (n c f) -> p n c f", n=B, c=2)
        junk = arena[:, 10240:11520].rearrange("p (a f) -> p a f", a=10)
        x2n = arena[:, 0:4096].rearrange("p (t f) -> p t f", f=P)
        kern = sb("kern", [P, 4, 10])
        OFF = [0, 1, 3, 6]

        def gau_pool(pool, ln):
            pool.wait_ge(ld["gau"], LD_GAU)
            for n in range(B):
                for i in range(2):
                    nc.gpsimd.tensor_scalar(rotqk[:, n, P * i:P * i + P], rot[:, n, :], cols[:, 3 + i:4 + i], 0.0,
                                            ALU.mult, ALU.add).then_inc(pr["gau"], 1)
                nc.gpsimd.tensor_copy(bias10[:, OFF[n]:OFF[n] + n + 1], wrel[:, 3 - n:4]).then_inc(pr["gau"], 1)
            nc.gpsimd.tensor_copy(wuvh[:], wuv[:]).then_inc(pr["gau"], 1)
            pool.wait_ge(pr["gau"], 13)
            nc.gpsimd.tensor_tensor(wuvl[:], wuv[:], wuvh[:], ALU.subtract).then_inc(pr["gau"], 1)

        def gau_shortcut(pool, ln):
            pool.wait_ge(*ln.at("norm", NT))
            nc.gpsimd.tensor_tensor(x[:], x[:], xn[:], ALU.add).then_inc(pr["gau_mm"], 1)
            pool.wait_ge(pr["gau_mm"], 1)
            nc.gpsimd.tensor_tensor(x[:], x[:], bo_b[:].unsqueeze(1).to_broadcast([P, NT, P]), ALU.add)\
                .then_inc(pr["gau_mm"], 1)

        def gau_tensor(pe, ln):
            pe.wait_ge(pr["gau"], 14)
            for n in range(B):
                for i in range(2):
                    last = nc.tensor.matmul(bank[2 + n // 2][0:1, 256 * (n % 2) + P * i:256 * (n % 2) + P * i + P],
                                            cols[:, 5 + i:6 + i], rot[:, n, :], start=True, stop=True)
            last.then_inc(au["rb"], 1)
            pe.wait_ge(*ln.at("low", NS))

            def front(j, par):
                pe.wait_ge(au["bs"], j + 1)
                xs = xnT.rearrange("p (n j f) -> p j n f", n=B, f=P)[:, ds(j, 1)]
                nc.tensor.matmul(bank[0][:], wbT[:], xs, start=True, stop=True).then_inc(au["b"], 1)
                for n in range(B):
                    ps = bank[1 + n % 2][:]
                    tok = ds(P * j + L * n, P)
                    pe.wait_ge(au["uv"], B * j + n + 1)
                    nc.tensor.matmul(ps, ones_bf[0:BR, 0:P], uvrows[:], start=True, stop=False)
                    nc.tensor.matmul(ps, xh[:, tok], wuvh[:], start=False, stop=False)
                    nc.tensor.matmul(ps, xl[:, tok], wuvh[:], start=False, stop=False)
                    nc.tensor.matmul(ps, xh[:, tok], wuvl[:], start=False, stop=True).then_inc(au["uvp"], 1)
                pe.wait_ge(au["bs"], j + 2)
                for n in range(B):
                    if n % 2 == 0:
                        pe.wait_ge(au["qkc"], 2 * j + n // 2 + 1)
                    ps = bank[3 + n // 2][:, 256 * (n % 2):256 * (n % 2) + 256]
                    nc.tensor.matmul(ps, ones_f[0:1, :], rotb[:, n, :], start=True, stop=False)
                    last = nc.tensor.matmul(ps, bs[:, par, P * n:P * n + P], rotqk[:, n, :], start=False, stop=True)
                    if n % 2:
                        last.then_inc(au["qkp"], 1)

            def back(j, par):
                pe.wait_ge(au["z"], j + 3)
                pe.wait_ge(au["ztc"], j + 1)
                for n in range(B):
                    for c in range(2):
                        o = 256 * (n % 2) + P * c
                        last = nc.tensor.transpose(bank[5 + n // 2][:, o:o + P], z[:, par, n, P * c:P * c + P], ident)
                last.then_inc(au["zt"], 1)
                pe.wait_ge(au["ztc"], j + 2)
                pe.wait_ge(au["add"], j + 1)
                for n in range(B):
                    for c in range(2):
                        last = nc.tensor.matmul(bank[7][:, P * n:P * n + P], zT[:, n, c], wo1[:, c, :],
                                                start=(c == 0), stop=(c == 1))
                last.then_inc(au["o"], 1)

            pe.wait_ge(au["rb"], 3)
            front(0, 0)
            with pe.Fori(0, NJ // 2 - 1) as pair:
                j = 2 * pair
                front(j + 1, 1)
                back(j, 0)
                front(j + 2, 0)
                back(j + 1, 1)
            front(NJ - 1, 1)
            back(NJ - 2, 0)
            back(NJ - 1, 1)

        def gau_scalar(act, ln):
            warm(act, ACT.Silu)
            act.wait_ge(au["rb"], 1)
            for i in range(2):
                nc.scalar.activation(rotb[:, 2 * i:2 * i + 2, :], bank[2 + i][0:1, :].rearrange("p (a f) -> p a f", a=2),
                                     ACT.Copy).then_inc(au["rb"], 1)

            def front(j, par):
                act.wait_ge(au["b"], j + 1)
                nc.scalar.activation(bs[:, par], bank[0][:], ACT.Silu, bias=cols[:, 2:3]).then_inc(au["bs"], 1)
                act.wait_ge(au["z"], j + 1)
                for n in range(B):
                    act.wait_ge(au["uvp"], B * j + n + 1)
                    nc.scalar.activation(uv[:, par, n], bank[1 + n % 2][:], ACT.Silu).then_inc(au["uv"], 1)
                for h in range(2):
                    act.wait_ge(au["qkp"], 2 * j + h + 1)
                    nc.scalar.activation(qk[:, par, 2 * h:2 * h + 2], bank[3 + h][:].rearrange("p (a f) -> p a f", a=2),
                                         ACT.Copy).then_inc(au["qkc"], 1)

            def back(j, par):
                act.wait_ge(au["zt"], j + 3)
                act.wait_ge(au["o"], j + 1)
                for h in range(2):
                    last = nc.scalar.activation(zT[:, 2 * h:2 * h + 2],
                                                bank[5 + h][:].rearrange("p (a c f) -> p a c f", a=2, c=2), ACT.Copy)
                last.then_inc(au["ztc"], 1)

            front(0, 0)
            with act.Fori(0, NJ // 2 - 1) as pair:
                j = 2 * pair
                front(j + 1, 1)
                back(j, 0)
                front(j + 2, 0)
                back(j + 1, 1)
            front(NJ - 1, 1)
            back(NJ - 2, 0)
            back(NJ - 1, 1)

        def gau_vector(dve, ln):
            for i, (q, v) in enumerate((("bs", 1), ("uv", 2), ("qkc", 2), ("z", 2), ("ztc", 1), ("add", 1),
                                        ("zt", 2), ("o", 1))):
                nc.vector.memset(credit[:, 16 + i:17 + i], 0.0).then_inc(au[q], v)
            dve.wait_ge(pr["gau_mm"], 2)
            qk10, t, r, kk = (kern[:, i, :] for i in range(4))
            STEPS = 9

            def front(j, par):
                at = j * STEPS
                dve.wait_ge(au["qkc"], 2 * j + 4)
                for n in range(B):
                    for m in range(n + 1):
                        i = OFF[n] + m
                        last = nc.vector.tensor_tensor_reduce(
                            out=junk[:, i], in0=qk[:, par, n, 0:P], in1=qk[:, par, m, P:2 * P], scale=1.0, scalar=0.0,
                            op0=ALU.mult, op1=ALU.add, accum_out=qk10[:, i:i + 1])
                last.then_inc(au["dve"], 1)
                dve.wait_ge(au["dve"], at + 1)
                nc.vector.scalar_tensor_tensor(t, qk10, 1.0 / 64, bias10[:], ALU.mult, ALU.add).then_inc(au["dve"], 1)
                dve.wait_ge(au["dve"], at + 2)
                nc.vector.tensor_scalar(r, t, 0.0, None, ALU.max).then_inc(au["dve"], 1)
                dve.wait_ge(au["dve"], at + 3)
                nc.vector.tensor_tensor(kk, r, r, ALU.mult).then_inc(au["dve"], 1)
                dve.wait_ge(au["dve"], at + 4)
                dve.wait_ge(au["uv"], B * j + B + 2)
                dve.wait_ge(au["zt"], j + 1)
                for m in range(B):
                    for n in range(m, B):
                        i = OFF[n] + m
                        v, w, zn = uv[:, par, m, 0:EH], kk[:, i:i + 1], z[:, par, n]
                        if m == 0:
                            last = nc.vector.tensor_scalar(zn, v, w, None, ALU.mult)
                        else:
                            last = nc.vector.scalar_tensor_tensor(zn, v, w, zn, ALU.mult, ALU.add)
                    last.then_inc(au["dve"], 1)
                    dve.wait_ge(au["dve"], at + 5 + m)
                nc.vector.tensor_tensor(z[:, par], z[:, par], uv[:, par, :, EH:2 * EH], ALU.mult).then_inc(au["z"], 1)
                nc.vector.memset(credit[:, 31:32], 0.0).then_inc(au["dve"], 1)
                dve.wait_ge(au["dve"], at + 9)

            def back(j, par):
                dve.wait_ge(au["o"], j + 2)
                xj = x[:].rearrange("p (n j) f -> p j n f", n=B)[:, ds(j, 1)]
                nc.vector.tensor_tensor(xj, xj, bank[7][:].rearrange("p (j n f) -> p j n f", j=1, n=B), ALU.add)\
                    .then_inc(au["add"], 1)

            front(0, 0)
            with dve.Fori(0, NJ // 2 - 1) as pair:
                j = 2 * pair
                front(j + 1, 1)
                back(j, 0)
                front(j + 2, 0)
                back(j + 1, 1)
            front(NJ - 1, 1)
            back(NJ - 2, 0)
            back(NJ - 1, 1)

        W0 = dict(FC=FC0, w1=(w1h0, w1l0), w2=(w2h0, w2l0), wr=wr0[:], bias=False, top2=False)
        W1 = dict(FC=FC1, w1=(w1h1, w1l1), w2=(w2h1, w2l1), wr=wr1[:], bias=True, top2=True)
        moe_done = lambda s: [s.at("comb", B)]
        xg, xb = cols[:, 0:1], cols[:, 1:2]

        ln0 = layernorm("ln0", x, xn, [(ld["x"], 16)], halves=False)
        moe0 = moe("moe0", ln0, 0, **W0)
        ln1 = layernorm("ln1", x, xn, moe_done(moe0))
        ln2 = layernorm("ln2", x, xn, [(gl["add"], NT)], halves=False)
        moe2 = moe("moe2", ln2, 1, **W0)
        ln3 = layernorm("ln3", x, xn, moe_done(moe2), halves=False)
        moe3 = moe("moe3", ln3, 2, **W1)
        ln4 = layernorm("ln4", x, xn, moe_done(moe3))
        ln5 = layernorm("ln5", xn, x2n, [ln4.at("norm", NT)], (xg, xb))
        ln6 = layernorm("ln6", x, xn, [(au["add"], NJ + 1)], halves=False)
        moe6 = moe("moe6", ln6, 3, **W1)
        stored = sem("stored")

        @block.sync
        def _(sp):
            load_sync(sp)
            moe_sync(sp, moe0, [(pr["w0l"], 2)])
            moe_sync(sp, moe2)
            moe_sync(sp, moe3)
            moe_sync(sp, moe6)
            sp.wait_ge(*moe6.at("comb", B))
            sp.dma_start(x_tiles(out), x[:]).then_inc(stored, 16)
            sp.wait_ge(stored, 16)

        @block.gpsimd
        def _(pool):
            nc.gpsimd.memset(ones_bf[:], 1.0).then_inc(pr["pool"], 1)
            nc.gpsimd.memset(ones_f[:], 1.0).then_inc(pr["pool"], 1)
            nc.gpsimd.memset(eps[:], 0.5).then_inc(pr["pool"], 1)
            for e in range(E):
                pool.dma_start(st_w2_0[:, e], d["w2_0"][e].rearrange("(c p) n -> p c n", p=P)).then_inc(scattered[e], 16)
            pool.wait_ge(ld["consts"], 32)
            nc.gpsimd.tensor_copy(strict_bf[:], consts[:, C_STRICT:C_STRICT + P]).then_inc(pr["pool"], 1)
            nc.gpsimd.tensor_copy(ident_bf[:], ident).then_inc(pr["pool"], 1)
            for i, (st, hi, lo, q, v) in enumerate(((st_w1_1, w1h1, w1l1, ld["w1"], LD_W1),
                                                    (st_w2_1, w2h1, w2l1, ld["w1b"], 16 * E))):
                pool.wait_ge(q, v)
                nc.gpsimd.tensor_copy(hi[:], st).then_inc(pr["w1h"], 1)
                pool.wait_ge(pr["w1h"], i + 1)
                nc.gpsimd.tensor_tensor(lo[:], st, hi[:], ALU.subtract).then_inc(pr["w1l"], 1)
            moe_pool(pool, moe0)
            rows_pool(pool)
            gau_pool(pool, ln4)
            moe_pool(pool, moe2)
            moe_pool(pool, moe3)
            gau_shortcut(pool, ln4)
            moe_pool(pool, moe6)

        @block.vector
        def _(dve):
            ln_vector(dve, ln0)

            def low_halves():
                dve.wait_ge(pr["w0h"], 2)
                nc.vector.tensor_tensor(w1l0[:], st_w1_0, w1h0[:], ALU.subtract).then_inc(pr["w0l"], 1)
                nc.vector.tensor_tensor(w2l0[:], st_w2_0, w2h0[:], ALU.subtract).then_inc(pr["w0l"], 1)
                dve.wait_ge(pr["w0l"], 2)
            moe_vector(dve, moe0, low_halves)
            ln_vector(dve, ln1)
            dve.wait_ge(pr["w1l"], 2)
            gla_vector(dve, ln1)
            ln_vector(dve, ln2)
            dve.wait_ge(pr["rows"], ROWS_DONE)
            moe_vector(dve, moe2)
            ln_vector(dve, ln3)
            moe_vector(dve, moe3)
            ln_vector(dve, ln4)
            ln_vector(dve, ln5)
            gau_vector(dve, ln5)
            ln_vector(dve, ln6)
            moe_vector(dve, moe6)

        @block.scalar
        def _(act):
            act.wait_ge(pr["pool"], 5)
            ln_scalar(act, ln0)

            def high_halves():
                act.wait_ge(ld["w0"], LD_W0)
                for e in range(E):
                    act.wait_ge(scattered[e], 16)
                nc.scalar.activation(w1h0[:], st_w1_0, ACT.Copy).then_inc(pr["w0h"], 1)
                nc.scalar.activation(w2h0[:], st_w2_0, ACT.Copy).then_inc(pr["w0h"], 1)
            moe_scalar(act, moe0, high_halves)
            ln_scalar(act, ln1)
            gla_scalar(act, ln1)
            ln_scalar(act, ln2)
            moe_scalar(act, moe2)
            ln_scalar(act, ln3)
            moe_scalar(act, moe3)
            ln_scalar(act, ln4)
            act.wait_ge(ld["gau"], LD_GAU)
            ln_scalar(act, ln5)
            gau_scalar(act, ln5)
            ln_scalar(act, ln6)
            moe_scalar(act, moe6)

        @block.tensor
        def _(pe):
            pe.wait_ge(ld["consts"], 32)
            ln_tensor(pe, ln0)
            moe_tensor(pe, moe0, [(pr["w0l"], 2)])
            ln_tensor(pe, ln1)
            gla_tensor(pe, ln1)
            ln_tensor(pe, ln2)
            moe_tensor(pe, moe2)
            ln_tensor(pe, ln3)
            pe.wait_ge(pr["w1l"], 2)
            pe.wait_ge(ld["w1"], LD_W1)
            pe.wait_ge(pr["rows"], ROWS_DONE)
            moe_tensor(pe, moe3)
            ln_tensor(pe, ln4)
            ln_tensor(pe, ln5)
            gau_tensor(pe, ln5)
            ln_tensor(pe, ln6)
            moe_tensor(pe, moe6)


def kernel(**inputs):
    import numpy as np
    import concourse.bacc as bacc
    from concourse.bass_utils import run_bass_kernel_spmd as run

    a = {k: np.asarray(v) for k, v in inputs.items()}
    c = np.ascontiguousarray
    f = np.float32
    k = np.arange(P)
    consts = np.zeros((P, C_END), f)
    consts[:, C_IDENT:C_IDENT + P] = np.eye(P, dtype=f)
    consts[:, C_NEGMASK:C_NEGMASK + P] = -(k[:, None] <= k[None, :]).astype(f)
    consts[:, C_STRICT:C_STRICT + P] = (k[:, None] < k[None, :]).astype(f)
    consts[:, C_SAMEEXP:C_SAMEEXP + P] = (k[:, None] % E == k[None, :] % E).astype(f)
    consts[:, C_RANK:C_RANK + E] = (E - np.arange(E)).astype(f)[None]
    consts[:, C_RESET:C_RESET + 256] = (np.arange(256) % 32 != 0).astype(f)[None]
    half = P // 2
    inv = (f(10000.0) ** (-np.arange(half, dtype=f) / f(half))).astype(f)
    rot = np.zeros((P, 4, P), f)
    i = np.arange(half)
    for n in range(4):
        ang = (f(n) * inv).astype(f)
        s, co = np.sin(ang).astype(f), np.cos(ang).astype(f)
        rot[i, n, i] = co
        rot[i + half, n, i] = -s
        rot[i + half, n, i + half] = co
        rot[i, n, i + half] = s
    T = a['L0_attn_x'].shape[0] * a['L0_attn_x'].shape[1]
    NT = T // P
    dest = (k[:, None, None] + P * np.arange(NT)[None, None] + T * np.arange(2)[None, :, None]).astype(np.int32)

    def pad(choices):
        n = (choices * NT + 2 * E) * P
        r = np.zeros((n, P + 2), f)
        r[:, P] = (choices * T + np.arange(n, dtype=np.int32)).view(f)
        return r

    uv = np.concatenate([a['L1_attn_bv'], a['L1_attn_bu']])
    brows = np.concatenate([a['L1_ffn_b2'], a['L1_ffn_b1'], np.zeros((E, uv.shape[0]), f)], 1)
    brows[0, -uv.shape[0]:] = uv
    F1 = a['L1_ffn_W1'].shape[2]
    selector = np.zeros((3, 32, E, F1), np.uint16)
    for e in range(E):
        selector[:, e, e] = 0x3f80
    selector = selector.reshape(96, E * F1)
    centre = a['L1_attn_w_rel'].shape[0] // 2
    arrays = {
        "x": a['L0_attn_x'], "consts": consts, "wg": a['L0_ffn_Wg'], "w1_0": a['L0_ffn_W1'], "w2_0": a['L0_ffn_W2'],
        "wqT": a['L0_attn_Wq'].T, "wkT": a['L0_attn_Wk'].T, "wvT": a['L0_attn_Wv'].T, "woT": a['L0_attn_Wo'].T,
        "norm_w": a['L0_attn_norm_w'][:, None],
        "w1_1": a['L1_ffn_W1'], "w2_1": a['L1_ffn_W2'], "wrT": a['L1_ffn_Wr'].T,
        "brows": brows, "selector": selector,
        "dest": dest, "starts": np.stack([2 * P * np.arange(NT + E), 8 ** (np.arange(NT + E) % 8)]).astype(f)[None], "pad1": pad(1), "pad2": pad(2),
        "wvT1": a['L1_attn_Wv'].T, "wuT": a['L1_attn_Wu'].T, "wbT": a['L1_attn_Wb'].T,
        "cols": np.stack([a['L1_attn_' + n] for n in ('ln_g', 'ln_b', 'bb', 'qqw', 'qkw', 'qqb', 'qkb')], 1),
        "rot": rot, "wo1": a['L1_attn_Wo'].T.reshape(2, P, P).transpose(1, 0, 2),
        "wrel": a['L1_attn_w_rel'][centre - 3:centre + 1], "bo": a['L1_attn_bo'],
    }
    nc = bacc.Bacc("TRN2", target_bir_lowering=False, num_devices=1)
    feed, d = {}, {}
    for name, v in arrays.items():
        v = c(v)
        feed[f"in_{name}"] = v
        d[name] = nc.dram_tensor(f"in_{name}", v.shape, mybir.dt.from_np(v.dtype), kind="ExternalInput").ap()
    shape = arrays["x"].shape
    out = nc.dram_tensor("out_x", shape, F32, kind="ExternalOutput").ap()
    program(nc, d, out)
    return run(nc, [feed], core_ids=[0]).results[0]["out_x"]
```

```python
from contextlib import ExitStack

import concourse.bass as bass
from concourse import mybir

F32 = mybir.dt.float32
BF16 = mybir.dt.bfloat16
I32 = mybir.dt.int32
ALU = mybir.AluOpType
ACT = mybir.ActivationFunctionType
AX = mybir.AxisListType.X
ds = bass.ds

P = 128
E = 8
NMAX = 512

C_IDENT = 0
C_NEGMASK = 128
C_STRICT = 256
C_SAMEEXP = 384
C_RANK = 512
C_RESET = 520
C_END = 520 + 256


def program(nc, d, out):
    B, L, D = d["x"].shape
    T = B * L
    NT = T // P
    NS = T // NMAX
    TPS = NMAX // P
    F0 = d["w1_0"].shape[2]
    F1 = d["w1_1"].shape[2]
    FC0, FC1 = F0 // P, F1 // P
    CAP = T // E
    EH = d["wuT"].shape[1]
    assert D == P and NT * E == 256 and EH == 2 * P and B == 4

    ctx = ExitStack()
    with ctx:
        def sb(name, shape, dt=F32):
            return ctx.enter_context(nc.sbuf_tensor(name, shape, dt))

        def sem(name):
            return ctx.enter_context(nc.semaphore(name))

        def sems(stage, *names):
            return {n: sem(f"{stage}_{n}") for n in names}

        class Signals(dict):
            def at(self, name, count):
                return self[name], self.base[name] + count

        kinds = {}

        def layer_sems(kind, totals):
            have = kinds.setdefault(kind, {})
            s = Signals()
            s.base = {}
            for n, total in totals.items():
                if n not in have:
                    have[n] = [sem(f"{kind}_{n}"), 0]
                s[n], s.base[n] = have[n]
                have[n][1] += total
            return s

        bank = [ctx.enter_context(nc.psum_tensor(f"bank{i}", [P, NMAX], F32)) for i in range(8)]

        x = sb("x", [P, NT, P])
        RW = P + 2
        rows = sb("rows", [P, NT, RW])
        xn = rows[:, :, 0:P]
        turned = sb("turned", [P, 8192])
        xnT = turned[:, 0:4096]
        xh = turned[:, 4096:6144].bitcast(BF16)
        xl = turned[:, 6144:8192].bitcast(BF16)
        arena = sb("arena", [P, 11520])
        consts = sb("consts", [P, C_END])
        ident = consts[:, C_IDENT:C_IDENT + P]
        ident_bf = sb("ident_bf", [P, P], BF16)
        negmask = consts[:, C_NEGMASK:C_NEGMASK + P]
        same_expert = consts[:, C_SAMEEXP:C_SAMEEXP + P]
        rank_w = consts[:, C_RANK:C_RANK + E]
        reset = consts[:, C_RESET:C_RESET + NT * E]
        ones_bf = sb("ones_bf", [P, P], BF16)
        ones_f = sb("ones_f", [P, P])
        strict_bf = sb("strict_bf", [P, P], BF16)
        eps = sb("eps", [P, 16])
        credit = sb("credit", [P, 32])

        w1h0, w1l0 = (sb(f"w1{h}0", [P, E, F0], BF16) for h in "hl")
        w2h0, w2l0 = (sb(f"w2{h}0", [P, E, FC0, P], BF16) for h in "hl")
        w1h1, w1l1 = (sb(f"w1{h}1", [P, E, F1], BF16) for h in "hl")
        w2h1, w2l1 = (sb(f"w2{h}1", [P, E, FC1, P], BF16) for h in "hl")
        wr0 = sb("wr0", [P, E])
        wr1 = sb("wr1", [P, E])
        BR = 96
        BW = P + F1 + 2 * EH
        brows = sb("brows", [BR, BW], BF16)
        b2rows, b1rows, uvrows = brows[:, 0:P], brows[:, P:P + F1], brows[:, P + F1:BW]
        selector_i = sb("selector", [BR, E * F1], mybir.dt.uint16)
        selector = selector_i[:].bitcast(BF16)
        wqT, wkT, wvT, woT = (sb(n, [P, P]) for n in ("wqT_s", "wkT_s", "wvT_s", "woT_s"))
        wvh, wvl = sb("wvh", [P, P], BF16), sb("wvl", [P, P], BF16)
        normw = sb("normw", [P, 1])
        woTn = sb("woTn", [P, P])
        wuv = sb("wuv", [P, 2 * EH])
        wuvh, wuvl = sb("wuvh", [P, 2 * EH], BF16), sb("wuvl", [P, 2 * EH], BF16)
        wbT = sb("wbT_s", [P, P])
        wo1 = sb("wo1", [P, EH // P, P])
        cols = sb("cols", [P, 8])
        rot = sb("rot", [P, B, P])
        rotqk = sb("rotqk", [P, B, 2 * P])
        wrel = sb("wrel", [P, 4])
        bias10 = sb("bias10", [P, 10])
        bo_b = sb("bo_b", [P, P])

        stats = sb("stats", [P, NT, 6])
        mean = sb("mean", [P, NT])
        nwt = sb("nwt", [P, 8, NT])
        rt = sb("rt", [P, 12, NT * E])
        rotb = rt[0:1, 0:B, :]
        small = sb("small", [P, 6, NT])
        pT = rt[:, 10, :]
        pjunk = rt[:, 11, :]
        srch = sb("srch", [P, 24])
        thr_in = sb("thr_in", [E, 2, P])
        thr = sb("thr", [P, 2 * E])
        eqb = sb("eqb", [P, NT * E], BF16)
        W = 2 * P
        PAIRS = {1: T // W + E, 2: 2 * T // W + E}
        SLOT_TILES = {k: 2 * n for k, n in PAIRS.items()}
        CHUNK = 8
        CP = CHUNK // 2
        BODY = 2 * CP
        dest = sb("dest", [P, 2, NT], I32)
        slot_i = sb("slot_i", [P, 2, NT], I32)
        per_e = sb("per_e", [P, 6, E])
        per_ei = sb("per_ei", [P, 2, E], I32)
        starts = sb("starts", [1, 2, PAIRS[2]])
        tcmp = rt[0:1, 2:5, :].rearrange("p a b -> p (a b)")[:, 0:PAIRS[2] * E].rearrange("p (t e) -> p t e", e=E)
        tsum = rt[0:1, 0, 0:2 * PAIRS[2]].rearrange("p (a t) -> p a t", a=2)
        pair_e = sb("pair_e", [1, PAIRS[2] // BODY], I32)
        out_idx = sb("out_idx", [P, CHUNK], I32)
        pool_junk = sb("pool_junk", [P, 2 * PAIRS[1] + 2 * PAIRS[2]], BF16)

        block = ctx.enter_context(nc.Block())

        ld = sems("load", "consts", "w0", "w1", "w1b", "consts2", "pad", "gla", "gau", "rows")
        pr = sems("prep", "pool", "w0h", "w0l", "w1h", "w1l", "gla", "gau", "gau_mm", "rows")

        st_w1_0 = arena[:, 0:E * F0].rearrange("p (e f) -> p e f", e=E)
        st_w2_0 = arena[:, E * F0:2 * E * F0].rearrange("p (e c n) -> p e c n", e=E, c=FC0)
        o = SLOT_TILES[1] * (P + 2)
        st_w1_1 = arena[:, o:o + E * F1].rearrange("p (e f) -> p e f", e=E)
        st_w2_1 = arena[:, o:o + E * F1].rearrange("p (e c n) -> p e c n", e=E, c=FC1)

        x_tiles = lambda ap: ap.rearrange("b (a p) n -> p (b a) n", p=P)

        def load_sync(sp):
            for b in range(B):
                sp.dma_start(x[:, NT // B * b:NT // B * (b + 1)], d["x"][b].rearrange("(a p) n -> p a n", p=P))\
                    .then_inc(loaded[b], 16)
            sp.dma_start(consts[:], d["consts"]).then_inc(ld["consts"], 16)
            sp.dma_start(wr0[:], d["wg"]).then_inc(ld["consts"], 16)
            sp.dma_start(st_w1_0, d["w1_0"].rearrange("e k f -> k e f")).then_inc(ld["w0"], 16)
            sp.dma_start(st_w1_1, d["w1_1"].rearrange("e k f -> k e f")).then_inc(ld["w1"], 16)
            sp.dma_start(wr1[:], d["wrT"]).then_inc(ld["w1"], 16)
            sp.dma_start(dest[:], d["dest"]).then_inc(ld["consts2"], 16)
            sp.dma_start(starts[:], d["starts"]).then_inc(ld["consts2"], 16)
            sp.dma_start(slots["moe0"], d["pad1"]).then_inc(ld["pad"], 16)
            sp.dma_start(selector_i[:], d["selector"]).then_inc(ld["consts2"], 16)
            for t, n in ((wqT, "wqT"), (wkT, "wkT"), (wvT, "wvT"), (woT, "woT"), (normw, "norm_w")):
                sp.dma_start(t[:], d[n]).then_inc(ld["gla"], 16)
            for t, n in ((wuv[:, 0:EH], "wvT1"), (wuv[:, EH:2 * EH], "wuT"), (wbT[:], "wbT"), (cols[:, 0:7], "cols"),
                         (rot[:], "rot"), (wo1[:], "wo1")):
                sp.dma_start(t, d[n]).then_inc(ld["gau"], 16)
            sp.dma_start(wrel[:], d["wrel"].partition_broadcast(P)).then_inc(ld["gau"], 16)
            sp.dma_start(bo_b[:], d["bo"].partition_broadcast(P)).then_inc(ld["gau"], 16)
            sp.wait_ge(pr["w1l"], 1)
            for e in range(E):
                sp.dma_start(st_w2_1[:, e], d["w2_1"][e].rearrange("(c p) n -> p c n", p=P)).then_inc(ld["w1b"], 16)

        def load_pads(sp):
            for name, n in (("moe2", "pad1"), ("moe3", "pad2"), ("moe6", "pad2")):
                sp.dma_start(slots[name], d[n]).then_inc(ld["pad"], 16)

        def rows_pool(pool):
            flat = rt[0:BR].rearrange("p a b -> p (a b)")
            f = flat[:, 0:BW]
            a, b = (flat[:, o:o + BW // 2].bitcast(BF16) for o in (BW, BW + BW // 2))
            n = 0

            def done(ins):
                nonlocal n
                n += 1
                ins.then_inc(pr["rows"], 1)
                pool.wait_ge(pr["rows"], n)

            done(nc.gpsimd.memset(brows[:], 0.0))
            done(nc.gpsimd.memset(f, 0.0))
            for q in (0, 32, 64):
                pool.dma_start(f[q:q + E], d["brows"]).then_inc(ld["rows"], 16)
            pool.wait_ge(ld["rows"], 16 * 3)
            done(nc.gpsimd.tensor_copy(a, f))
            done(nc.gpsimd.tensor_tensor(f, f, a, ALU.subtract))
            done(nc.gpsimd.tensor_copy(b, f))
            done(nc.gpsimd.tensor_tensor(f, f, b, ALU.subtract))
            for q, part in ((0, a), (32, b), (64, f)):
                done(nc.gpsimd.tensor_copy(brows[q:q + E], part[q:q + E]))
        ROWS_DONE = 2 + 4 + 3

        LD_W0 = 16
        LD_W1 = 16 * 2
        LD_GAU = 16 * 8
        LD_GLA = 16 * 5

        def layernorm(src, dst, source_ready, gb=None, halves=True, turn=True):
            s = layer_sems("ln", dict(stat=NT, aggr=6, rsqrt=1 + RSQRT_STEPS, norm=NT, turned=NS * turn,
                                      copied=NS * turn * (1 + halves), low=NS * halves))
            s.update(begun=False, src=src, dst=dst, ready=source_ready, gb=gb, halves=halves, copies=2 if halves else 1)
            return s

        def inverse_sqrt(dve, chain, n0, value, res):
            t, y, a, b = (nwt[:, i, :] for i in range(1, 5))
            n = n0

            def done(ins):
                nonlocal n
                n += 1
                ins.then_inc(chain, 1)
                dve.wait_ge(chain, n)

            done(nc.vector.tensor_scalar(t.bitcast(I32), value.bitcast(I32), 1, None, ALU.logical_shift_right))
            done(nc.vector.tensor_scalar(y.bitcast(I32), t.bitcast(I32), -1.0, float(0x5F3759DF), ALU.mult, ALU.add))
            for i in range(4):
                done(nc.vector.tensor_tensor(a, y, y, ALU.mult))
                done(nc.vector.scalar_tensor_tensor(b, a, -0.5, value, ALU.mult, ALU.mult))
                done(nc.vector.scalar_tensor_tensor(res if i == 3 else y, b, 1.5, y, ALU.add, ALU.mult))
            return n
        RSQRT_STEPS = 14

        def ln_stats(s, tiles):
            for t in tiles:
                nc.vector.bn_stats(stats[:, t, :], s["src"][:, t, :]).then_inc(s["stat"], 1)

        def ln_vector(dve, s):
            src, dst = s["src"], s["dst"]
            if not s["begun"]:
                for q, v in s["ready"]:
                    dve.wait_ge(q, v)
                ln_stats(s, range(NT))
            dve.wait_ge(*s.at("stat", NT))
            var, rs, sums, diff, msum = nwt[:, 0, :], nwt[:, 5, :], nwt[:, 6, :], nwt[:, 7, :], nwt[:, 1, :]
            me, mo = stats[:, :, 1], stats[:, :, 4]
            nc.vector.tensor_tensor(sums, me, mo, ALU.add).then_inc(s["aggr"], 1)
            nc.vector.tensor_tensor(diff, me, mo, ALU.subtract).then_inc(s["aggr"], 1)
            nc.vector.tensor_tensor(msum, stats[:, :, 2], stats[:, :, 5], ALU.add).then_inc(s["aggr"], 1)
            dve.wait_ge(*s.at("aggr", 3))
            nc.vector.tensor_scalar(mean[:], sums, 0.5, None, ALU.mult).then_inc(s["aggr"], 1)
            nc.vector.scalar_tensor_tensor(nwt[:, 2, :], diff, 0.25, diff, ALU.mult, ALU.mult).then_inc(s["aggr"], 1)
            nc.vector.tensor_scalar(nwt[:, 3, :], msum, 1.0 / P, 1e-5, ALU.mult, ALU.add).then_inc(s["aggr"], 1)
            dve.wait_ge(*s.at("aggr", 6))
            nc.vector.tensor_tensor(var, nwt[:, 2, :], nwt[:, 3, :], ALU.add).then_inc(s["rsqrt"], 1)
            dve.wait_ge(*s.at("rsqrt", 1))
            inverse_sqrt(dve, s["rsqrt"], s.base["rsqrt"] + 1, var, rs)
            for t in range(NT):
                nc.vector.tensor_scalar(dst[:, t, :], src[:, t, :], mean[:, t:t + 1], rs[:, t:t + 1],
                                        ALU.subtract, ALU.mult).then_inc(s["norm"], 1)
            if not s["halves"]:
                return
            for i in range(NS):
                dve.wait_ge(*s.at("copied", 2 * i + 2))
                o = slice(NMAX * i, NMAX * (i + 1))
                nc.vector.tensor_tensor(xl[:, o], xnT[:, o], xh[:, o], ALU.subtract).then_inc(s["low"], 1)

        def ln_tensor(pe, s, router=None):
            def logits(i):
                pe.wait_ge(*s.at("copied", s["copies"] * (i + 1)))
                for t in range(TPS * i, TPS * (i + 1)):
                    last = nc.tensor.matmul(bank[6][:, E * t:E * t + E], xnT[:, P * t:P * t + P], router,
                                            start=True, stop=True)
                return last

            for i in range(NS):
                pe.wait_ge(*s.at("norm", TPS * (i + 1)))
                if i >= 2:
                    pe.wait_ge(*s.at("copied", s["copies"] * (i - 1)))
                for j in range(TPS):
                    last = nc.tensor.transpose(bank[i % 2][:, P * j:P * (j + 1)], s["dst"][:, TPS * i + j, :], ident)
                last.then_inc(s["turned"], 1)
                if router is not None and i >= 2:
                    logits(i - 2)
            if router is not None:
                logits(NS - 2)
                return logits(NS - 1)

        def ln_scalar(act, s):
            for i in range(NS):
                act.wait_ge(*s.at("turned", i + 1))
                for t in (xnT, xh)[0:s["copies"]]:
                    o = t[:, NMAX * i:NMAX * (i + 1)]
                    if s["gb"]:
                        ins = nc.scalar.activation(o, bank[i % 2][:], ACT.Identity, bias=s["gb"][1], scale=s["gb"][0])
                    else:
                        ins = nc.scalar.activation(o, bank[i % 2][:], ACT.Identity)
                    ins.then_inc(s["copied"], 1)

        warm_sem = sem("table_warm")
        warmed = [0]

        def warm(act, function):
            warmed[0] += 1
            c = warmed[0]
            nc.scalar.activation(eps[:, c:c + 1], eps[:, 0:1], function).then_inc(warm_sem, 1)

        R_P, R_GT, R_SEL, R_PM, R_TOT, R_INC, R_A, R_B, R_C, R_D, R_K1 = range(11)

        def v3(i):
            return rt[:, i, :].rearrange("p (t e) -> p t e", e=E)

        def over_e(a):
            return a.unsqueeze(2).to_broadcast([P, NT, E])

        def over_t(a):
            return a.unsqueeze(1).to_broadcast([P, NT, E])

        RINGS = dict(xT=2, act=2, low=2, down=4, y=2)
        RING = 2
        SEARCH = 15
        SK = 5

        scattered = [sem(f"scattered{k}") for k in range(CHUNK)]
        loaded = [sem(f"loaded{b}") for b in range(B)]
        SCATTERS = [1]
        YSB = SLOT_TILES[2] * RW
        slots, ydram = {}, {}
        for name, k in (("moe0", 1), ("moe2", 1), ("moe3", 2), ("moe6", 2)):
            n = SLOT_TILES[k]
            slots[name] = nc.dram_tensor(f"slots_{name}", [n * P, RW], F32, kind="Internal").ap()
            ydram[name] = nc.dram_tensor(f"y_{name}", [k * T + n * P, P], F32, kind="Internal").ap()
            SCATTERS.append(SCATTERS[-1] + n // CHUNK)

        def moe(stage, ln, index, FC, w1, w2, wr, bias, top2):
            K, n = (2 if top2 else 1), SLOT_TILES[2 if top2 else 1]
            s = layer_sems("moe", dict(logits=1, exp=1, ptT=2 - K, count=(2 - K) * (SEARCH + 1), thr=2 - K,
                                       prefix=3 - K, placed=3, cols=2 if K == 1 else 1 + 2 * B, rows=16 * (n // CHUNK),
                                       split=n // CHUNK, turned=n // 2, up=n // 2, comb=B,
                                       **{f"sent{g}": 16 * K * (NT // B) for g in range(B)},
                                       **{q: RINGS[q] + n // 2 for q in RINGS}))
            s["route"] = sem(f"{stage}_route")
            s.base["route"] = 0
            s.update(ln=ln, FC=FC, w1=w1, w2=w2, wr=wr, bias=bias, top2=top2, index=index)
            s["K"] = 2 if top2 else 1
            s["tiles"] = SLOT_TILES[s["K"]]
            s["before"] = SCATTERS[index]
            s["slots"], s["ydram"] = slots[stage], ydram[stage]
            s["pads"] = 16 if index == 0 else 16 * 4
            s["y_before"] = 16 * (1, 2, 3, 5)[index]
            s["in"] = arena[:, 0:s["tiles"] * RW].rearrange("p (t r) -> p t r", r=RW)
            s["pairs"] = s["tiles"] // 2
            s["ybuf"] = arena[:, 0:s["K"] * 4096].rearrange("p (k t n) -> p k t n", k=s["K"], n=P)
            o = 0

            def take(words):
                nonlocal o
                o += words
                return turned[:, o - words:o]
            s["xs"] = take(2 * CHUNK * P).bitcast(BF16).rearrange("p (h k t n) -> p h k t n", h=2, k=2, t=CHUNK)
            s["hh"], s["hl"] = (take(2 * FC * W).bitcast(BF16).rearrange("p (k n) -> p k n", k=4) for i in range(2))
            s["h32"] = take(2 * FC * W).rearrange("p (k n) -> p k n", k=2)
            s["xT_t"] = rt[:, 6:8, :].bitcast(BF16)
            s["ysb"] = arena[:, YSB:YSB + CHUNK * P].rearrange("p (k n) -> p k n", k=CHUNK)
            return s

        def moe_tensor(pe, s, weights=()):
            FC = s["FC"]
            router = bank[6]
            ln_tensor(pe, s["ln"], s["wr"]).then_inc(s["logits"], 1)

            if not s["top2"]:
                pe.wait_ge(*s.at("route", 5))
                for k in range(2):
                    last = nc.tensor.transpose(bank[7][:, P * k:P * k + P], rt[:, R_P, P * k:P * k + P], ident)
                last.then_inc(s["ptT"], 1)
                for i in range(SEARCH):
                    pe.wait_ge(*s.at("route", ROUTE_SEARCH + SK * i + 2))
                    nc.tensor.matmul(bank[7][:, 256:259], same_expert, srch[:, 8:11], start=True, stop=True)\
                        .then_inc(s["count"], 1)
                end = ROUTE_SEARCH + SK * SEARCH
                pe.wait_ge(*s.at("route", end + 1))
                nc.tensor.matmul(bank[7][:, 256:257], same_expert, srch[:, 8:9], start=True, stop=True)\
                    .then_inc(s["count"], 1)
                pe.wait_ge(*s.at("route", end + 4))
                for k in range(2):
                    last = nc.tensor.transpose(bank[7][:, 260 + E * k:260 + E * k + E], thr_in[:, k, :], ident[0:E, 0:E])
                last.then_inc(s["thr"], 1)
                pe.wait_ge(*s.at("route", end + 7))
                nc.tensor.matmul(router[:, 0:256], strict_bf[:], eqb[:], start=True, stop=True)
                nc.tensor.matmul(router[:, 256:512], ones_bf[:], eqb[:], start=True, stop=True).then_inc(s["prefix"], 1)
            pe.wait_ge(*s.at("placed", 1))
            nc.tensor.matmul(router[:, 0:256], strict_bf[:], eqb[:], start=True, stop=True)
            nc.tensor.matmul(router[:, 256:512], ones_bf[:], eqb[:], start=True, stop=True).then_inc(s["prefix"], 1)

            (w1h, w1l), (w2h, w2l) = s["w1"], s["w2"]
            pairs = s["pairs"]
            pe.wait_ge(*s.at("placed", 3))
            for q, v in weights:
                pe.wait_ge(q, v)

            def packed(c):
                return pe.value_load(pair_e[0:1, ds(c, 1)], min_val=0, max_val=E ** BODY - 1)

            def expert(packs, k):
                return pe.snap((packs[k // BODY] // E ** (k % BODY)) % E * (FC * P))

            def turn(t, k):
                if k % CP == 0:
                    pe.wait_ge(*s.at("split", t // CP + 1))
                pe.wait_ge(*s.at("xT", t + 1))
                o = bank[7 * (k % 2)][:].bitcast(BF16)
                for h in range(2):
                    for j in range(2):
                        last = nc.tensor.transpose(o[:, W * h + P * j:W * h + P * j + P],
                                                   s["xs"][:, h, k // CP % 2, 2 * (k % CP) + j, :], ident_bf[:])
                last.then_inc(s["turned"], 1)

            def up(t, k, e):
                r = k % 2
                xT = s["xT_t"][:, r]
                pe.wait_ge(*s.at("xT", t + 1 + RING))
                pe.wait_ge(*s.at("act", t + 1))
                for u in range(FC):
                    o = bank[1 + 2 * r + u // 2][:, W * (u % 2):W * (u % 2) + W]
                    wh, wl = (w[:].rearrange("p e f -> p (e f)")[:, ds(e + P * u, P)] for w in (w1h, w1l))
                    if s["bias"]:
                        nc.tensor.matmul(o, b1rows[:, P * u:P * u + P], selector[:, ds(e, W)], start=True, stop=False)
                    nc.tensor.matmul(o, wh, xT[:, 0:W], start=not s["bias"], stop=False)
                    nc.tensor.matmul(o, wh, xT[:, W:2 * W], start=False, stop=False)
                    last = nc.tensor.matmul(o, wl, xT[:, 0:W], start=False, stop=True)
                last.then_inc(s["up"], 1)

            def down(t, k, e):
                r = k % 2
                y = [bank[5 + r][:, P * j:P * j + P] for j in range(2)]
                pe.wait_ge(*s.at("y", t + 1))
                pe.wait_ge(*s.at("low", t + 1 + RING))
                if s["bias"]:
                    for j in range(2):
                        nc.tensor.matmul(y[j], selector[:, ds(e, P)], b2rows, start=(j == 0), stop=False)
                for u in range(FC):
                    hh, hl = ([s[n][:, k % 4, W * u + P * j:W * u + P * j + P] for j in range(2)] for n in ("hh", "hl"))
                    wh, wl = (w[:].rearrange("p e c n -> p (e c n)")[:, ds(e + P * u, P)] for w in (w2h, w2l))
                    for j in range(2):
                        nc.tensor.matmul(y[j], hh[j], wh, start=(u + j == 0 and not s["bias"]), stop=False)
                        nc.tensor.matmul(y[j], hl[j], wh, start=False, stop=False)
                    for j in range(2):
                        last = nc.tensor.matmul(y[j], hh[j], wl, start=False, stop=(u == FC - 1 and j == 1))
                last.then_inc(s["down"], 1)

            turn(0, 0)
            turn(1, 1)
            packs = [packed(0)]
            up(0, 0, expert(packs, 0))
            turn(2, 2)
            up(1, 1, expert(packs, 1))
            with pe.Fori(0, pairs // BODY - 1) as c:
                packs = [packed(c), packed(c + 1)]
                e = [expert(packs, 0), expert(packs, 1)]
                for k in range(BODY):
                    t = BODY * c + k
                    turn(t + 3, k + 3)
                    e.append(expert(packs, k + 2))
                    up(t + 2, k + 2, e[k + 2])
                    down(t, k, e[k])
            packs = [packed(pairs // BODY - 1)]
            e = [expert(packs, k) for k in range(BODY)]
            for k in range(BODY):
                t = pairs - BODY + k
                if k + 3 < BODY:
                    turn(t + 3, k + 3)
                if k + 2 < BODY:
                    up(t + 2, k + 2, e[k + 2])
                down(t, k, e[k])

        def moe_scalar(act, s, meanwhile=lambda: None):
            FC = s["FC"]
            act.wait_ge(*s.at("route", 2))
            nc.scalar.activation(rt[:, R_A, :], rt[:, R_B, :], ACT.Exp).then_inc(s["exp"], 1)
            meanwhile()
            warm(act, ACT.Gelu)
            act.wait_ge(*s.at("placed", 3))
            with act.Fori(0, s["pairs"] // 4) as four:
                for k in range(4):
                    t, r = 4 * four + k, k % 2
                    act.wait_ge(*s.at("up", t + 1))
                    act.wait_ge(*s.at("low", t + 1))
                    act.wait_ge(*s.at("down", t + 1))
                    for i in range(FC // 2):
                        o = slice(NMAX * i, NMAX * (i + 1))
                        nc.scalar.activation(s["h32"][:, r, o], bank[1 + 2 * r + i][:], ACT.Gelu)
                        last = nc.scalar.activation(s["hh"][:, k, o], bank[1 + 2 * r + i][:], ACT.Gelu)
                    last.then_inc(s["act"], 1)

        ROUTE_SEARCH = 7

        def moe_vector(dve, s, meanwhile=lambda: None, next_ln=None):
            FC, chain = s["FC"], s["route"]
            n = 0

            def done(ins):
                nonlocal n
                n += 1
                ins.then_inc(chain, 1)
                dve.wait_ge(chain, n)

            for q, ring in RINGS.items():
                nc.vector.memset(srch[:, 23:24], 0.0).then_inc(s[q], ring)
                dve.wait_ge(*s.at(q, ring))

            lg = bank[6][:, 0:256].rearrange("p (t e) -> p t e", e=E)
            p, p3 = rt[:, R_P, :], v3(R_P)
            dve.wait_ge(*s.at("logits", 1))
            done(nc.vector.tensor_reduce(small[:, 0, :], lg, AX, ALU.max))
            done(nc.vector.tensor_tensor(v3(R_B), lg, over_e(small[:, 0, :]), ALU.subtract))
            dve.wait_ge(*s.at("exp", 1))
            done(nc.vector.tensor_reduce(small[:, 1, :], v3(R_A), AX, ALU.add))
            done(nc.vector.reciprocal(small[:, 2, :], small[:, 1, :]))
            done(nc.vector.tensor_tensor(p3, v3(R_A), over_e(small[:, 2, :]), ALU.mult))

            def first_largest(value, maximum, onehot, sc_a, sc_b):
                done(nc.vector.tensor_reduce(maximum, v3(value), AX, ALU.max))
                done(nc.vector.tensor_tensor(v3(sc_a), v3(value), over_e(maximum), ALU.is_equal))
                done(nc.vector.tensor_tensor(v3(sc_b), v3(sc_a), over_t(rank_w), ALU.mult))
                done(nc.vector.tensor_reduce(small[:, 5, :], v3(sc_b), AX, ALU.max))
                done(nc.vector.tensor_tensor(v3(onehot), v3(sc_b), over_e(small[:, 5, :]), ALU.is_equal))

            def prefix_sums(ready):
                dve.wait_ge(*s.at("prefix", ready))
                tot = rt[:, R_TOT, :]
                done(nc.vector.tensor_copy(tot.rearrange("p (e t) -> p e t", e=E),
                                           bank[6][:, 256:512].rearrange("p (t e) -> p e t", e=E)))
                done(nc.vector.tensor_tensor_scan(rt[:, R_INC, :], reset, tot, 0.0, ALU.mult, ALU.add))
                done(nc.vector.tensor_tensor(rt[:, R_A, :], rt[:, R_INC, :], tot, ALU.subtract))
                done(nc.vector.tensor_tensor(v3(R_B), rt[:, R_A, :].rearrange("p (e t) -> p t e", e=E),
                                             bank[6][:, 0:256].rearrange("p (t e) -> p t e", e=E), ALU.add))

            if s["top2"]:
                first_largest(R_P, small[:, 3, :], R_K1, R_A, R_B)
                done(nc.vector.scalar_tensor_tensor(rt[:, R_C, :], rt[:, R_K1, :], -2.0, p, ALU.mult, ALU.add))
                first_largest(R_C, small[:, 4, :], R_D, R_A, R_B)
                done(nc.vector.tensor_tensor(eqb[:], rt[:, R_K1, :], rt[:, R_D, :], ALU.add))
                prefixes = 0
            else:
                i32 = lambda a: a.bitcast(I32)
                cand, T_, bits, cnt, kept, need = (srch[:, a:b] for a, b in
                                                   ((0, 3), (3, 4), (4, 7), (8, 11), (12, 16), (16, 17)))
                done(nc.vector.memset(i32(T_), 0))
                for k in range(3):
                    last = nc.vector.memset(i32(bits[:, k:k + 1]), (k + 1) << 28)
                done(last)
                assert n == ROUTE_SEARCH
                dve.wait_ge(*s.at("ptT", 1))
                nc.vector.tensor_copy(pT, bank[7][:, 0:256]).then_inc(s["cols"], 1)
                dve.wait_ge(*s.at("cols", 1))
                for i in range(SEARCH):
                    base = i * SK + ROUTE_SEARCH
                    nc.vector.tensor_tensor(i32(cand), i32(T_).to_broadcast([P, 3]), i32(bits), ALU.bitwise_or)\
                        .then_inc(chain, 1)
                    dve.wait_ge(chain, base + 1)
                    for k in range(3):
                        last = nc.vector.tensor_scalar(rt[:, 7 + k, :] if k else pjunk, pT, cand[:, k:k + 1], None,
                                                       ALU.is_ge, ALU.add, accum_out=cnt[:, k:k + 1])
                    last.then_inc(chain, 1)
                    nc.vector.tensor_scalar(i32(bits), i32(bits), 2, None, ALU.logical_shift_right).then_inc(chain, 1)
                    nc.vector.tensor_copy(kept[:, 3:4], T_)
                    dve.wait_ge(*s.at("count", i + 1))
                    nc.vector.scalar_tensor_tensor(kept[:, 0:3], bank[7][:, 256:259], CAP - 0.5, cand,
                                                   ALU.is_ge, ALU.mult).then_inc(chain, 1)
                    dve.wait_ge(chain, base + 4)
                    nc.vector.tensor_reduce(T_, kept, AX, ALU.max).then_inc(chain, 1)
                    dve.wait_ge(chain, base + 5)
                n += SK * SEARCH
                done(nc.vector.tensor_scalar(pjunk, pT, T_, None, ALU.is_gt, ALU.add, accum_out=cnt[:, 0:1]))
                dve.wait_ge(*s.at("count", SEARCH + 1))
                done(nc.vector.tensor_scalar(need, bank[7][:, 256:257], -1.0, float(CAP), ALU.mult, ALU.add))
                done(nc.vector.tensor_copy(thr_in[:, 0, :], T_[0:E].to_broadcast([E, P])))
                done(nc.vector.tensor_copy(thr_in[:, 1, :], need[0:E].to_broadcast([E, P])))
                dve.wait_ge(*s.at("thr", 1))
                done(nc.vector.tensor_copy(thr[:], bank[7][:, 260:260 + 2 * E]))
                done(nc.vector.tensor_tensor(v3(R_GT), p3, over_t(thr[:, 0:E]), ALU.is_gt))
                done(nc.vector.tensor_tensor(eqb[:].rearrange("p (t e) -> p t e", e=E), p3, over_t(thr[:, 0:E]),
                                             ALU.is_equal))
                prefix_sums(1)
                done(nc.vector.tensor_tensor(v3(R_C), v3(R_B), over_t(thr[:, E:2 * E]), ALU.is_lt))
                done(nc.vector.tensor_tensor(rt[:, R_D, :], rt[:, R_C, :], eqb[:], ALU.mult))
                done(nc.vector.tensor_tensor(rt[:, R_SEL, :], rt[:, R_D, :], rt[:, R_GT, :], ALU.add))
                done(nc.vector.tensor_tensor(rt[:, R_A, :], rt[:, R_SEL, :], p, ALU.mult))
                done(nc.vector.scalar_tensor_tensor(rt[:, R_PM, :], rt[:, R_SEL, :], 1.0, rt[:, R_A, :],
                                                    ALU.subtract, ALU.add))
                done(nc.vector.tensor_reduce(small[:, 3, :], v3(R_SEL), AX, ALU.max))
                done(nc.vector.tensor_scalar(small[:, 4, :], small[:, 3, :], -1.0, 1.0, ALU.mult, ALU.add))
                done(nc.vector.tensor_tensor(v3(R_B), p3, over_e(small[:, 4, :]), ALU.mult))
                done(nc.vector.tensor_tensor(v3(R_C), v3(R_B), over_e(small[:, 3, :]), ALU.subtract))
                done(nc.vector.tensor_tensor(rt[:, R_D, :], rt[:, R_C, :], rt[:, R_PM, :], ALU.max))
                first_largest(R_D, small[:, 4, :], R_K1, R_A, R_B)
                done(nc.vector.tensor_copy(eqb[:], rt[:, R_K1, :]))
                prefixes = 1

            nc.vector.memset(srch[:, 23:24], 0.0).then_inc(s["placed"], 1)
            prefix_sums(prefixes + 1)
            padded, first, end, slot_end = (per_e[:, i, :] for i in range(4))
            total = rt[:, R_INC, :].rearrange("p (e t) -> p e t", e=E)[:, :, NT - 1]
            bits_w = W.bit_length() - 1
            done(nc.vector.tensor_scalar(per_ei[:, 0, :], total, float(W - 1), None, ALU.add))
            done(nc.vector.tensor_scalar(per_ei[:, 1, :], per_ei[:, 0, :], bits_w, bits_w, ALU.logical_shift_right,
                                         ALU.logical_shift_left))
            done(nc.vector.tensor_copy(padded, per_ei[:, 1, :]))
            done(nc.vector.tensor_tensor_scan(end, ones_f[:, 0:E], padded, 0.0, ALU.mult, ALU.add))
            done(nc.vector.tensor_tensor(first, end, padded, ALU.subtract))
            done(nc.vector.tensor_tensor(v3(R_C), v3(R_B), over_t(first), ALU.add))
            for k, onehot in ((0, R_K1), (1, R_D))[0:s["K"]]:
                done(nc.vector.tensor_tensor(rt[:, R_A, :], rt[:, R_C, :], rt[:, onehot, :], ALU.mult))
                done(nc.vector.tensor_reduce(small[:, 1 + k, :], v3(R_A), AX, ALU.add))
                done(nc.vector.tensor_copy(slot_i[:, k, :], small[:, 1 + k, :]))
                done(nc.vector.scalar_tensor_tensor(rt[:, R_B, :], p, 0.5, rt[:, onehot, :], ALU.mult, ALU.mult))
                done(nc.vector.tensor_reduce(small[:, 3 + k, :], v3(R_B), AX, ALU.add))
            gates = [small[:, 3, :], small[:, 4, :]]

            def columns(k, tiles):
                nc.vector.tensor_copy(rows[:, tiles, P].bitcast(I32), dest[:, k, tiles])
                nc.vector.tensor_copy(rows[:, tiles, P + 1], gates[k][:, tiles]).then_inc(s["cols"], 1)

            dve.wait_ge(ld["consts2"], 48)
            columns(0, slice(0, NT))
            pairs = s["pairs"]
            done(nc.vector.tensor_tensor(tcmp[:, 0:pairs], starts[:, 0, 0:pairs].unsqueeze(2).to_broadcast([1, pairs, E]),
                                         end[0:1].unsqueeze(1).to_broadcast([1, pairs, E]), ALU.is_ge))
            done(nc.vector.tensor_reduce(tsum[:, 0, 0:pairs], tcmp[:, 0:pairs], AX, ALU.add))
            done(nc.vector.tensor_scalar(tsum[:, 1, 0:pairs], tsum[:, 0, 0:pairs], float(E - 1), None, ALU.min))
            done(nc.vector.tensor_tensor(tsum[:, 0, 0:pairs], tsum[:, 1, 0:pairs], starts[:, 1, 0:pairs], ALU.mult))
            done(nc.vector.tensor_reduce(tsum[:, 1, 0:pairs // BODY],
                                         tsum[:, 0, 0:pairs].rearrange("p (c k) -> p c k", k=BODY), AX, ALU.add))
            nc.vector.tensor_copy(pair_e[:, 0:pairs // BODY], tsum[:, 1, 0:pairs // BODY]).then_inc(s["placed"], 2)
            if s["K"] == 2:
                for g in range(B):
                    dve.wait_ge(*s.at(f"sent{g}", 16 * (NT // B)))
                    columns(1, slice(NT // B * g, NT // B * (g + 1)))

            def split(c):
                dve.wait_ge(*s.at("rows", 16 * c + 16))
                src = s["in"][:, ds(CHUNK * c, CHUNK), 0:P]
                h, l = (s["xs"][:, i, ds(c % 2, 1)].squeeze(1) for i in range(2))
                nc.vector.tensor_copy(h, src).then_inc(chain, 1)
                dve.wait_ge(chain, c + (n + 1))
                nc.vector.tensor_tensor(l, src, h, ALU.subtract).then_inc(s["split"], 1)

            def copy_turned(t, k):
                dve.wait_ge(*s.at("turned", t + 1))
                if k >= 2:
                    dve.wait_ge(*s.at("up", t - 1))
                nc.vector.tensor_copy(s["xT_t"][:, k % 2], bank[7 * (k % 2)][:].bitcast(BF16)[:, 0:2 * W])\
                    .then_inc(s["xT"], 1)

            def low(t, k):
                r = k % 2
                dve.wait_ge(*s.at("act", t + 1 + RING))
                nc.vector.tensor_tensor(s["hl"][:, k % 4], s["h32"][:, r], s["hh"][:, k % 4], ALU.subtract)\
                    .then_inc(s["low"], 1)

            def finish(t, k):
                dve.wait_ge(*s.at("down", t + 1 + RINGS["down"]))
                for j in range(2):
                    slot, tile = 2 * (k % CP) + j, 2 * t + j
                    dve.wait_ge(scattered[slot], 16 * (s["before"] + t // CP))
                    nc.vector.tensor_copy(out_idx[:, slot:slot + 1], s["in"][:, ds(tile, 1), P].bitcast(I32))
                    last = nc.vector.tensor_scalar(s["ysb"][:, slot], bank[5 + k % 2][:, P * j:P * j + P],
                                                   s["in"][:, ds(tile, 1), P + 1], None, ALU.mult)
                last.then_inc(s["y"], 1)

            meanwhile()
            split(0)
            copy_turned(0, 0)
            copy_turned(1, 1)
            low(0, 0)
            copy_turned(2, 2)
            with dve.Fori(0, pairs // BODY - 1) as c:
                for k in range(BODY):
                    t = BODY * c + k
                    if k % CP == 0:
                        split(2 * c + k // CP + 1)
                    copy_turned(t + 3, k + 3)
                    low(t + 1, k + 1)
                    finish(t, k)
            for k in range(BODY):
                t = pairs - BODY + k
                if k == 0:
                    split(pairs // CP - 1)
                if k + 3 < BODY:
                    copy_turned(t + 3, k + 3)
                if k + 1 < BODY:
                    low(t + 1, k + 1)
                finish(t, k)

            for b in range(B):
                tb = slice(NT // B * b, NT // B * (b + 1))
                for k in range(s["K"]):
                    dve.wait_ge(loaded[b], s["y_before"] + 16 * s["K"])
                    ins = nc.vector.tensor_tensor(x[:, tb], x[:, tb], s["ybuf"][:, k, tb], ALU.add)
                    if k < s["K"] - 1:
                        ins.then_inc(s["cols"], 1)
                        dve.wait_ge(*s.at("cols", 1 + B + b + 1))
                ins.then_inc(s["comb"], 1)
                if next_ln:
                    dve.wait_ge(*s.at("comb", b + 1))
                    ln_stats(next_ln, range(NT)[tb])
            if next_ln:
                next_ln["begun"] = True

        def moe_sync(sp, s, place_free=()):
            for g in range(B):
                sp.wait_ge(*s.at(f"sent{g}", 16 * s["K"] * (NT // B)))
            for q, v in place_free:
                sp.wait_ge(q, v)
            for c in range(s["tiles"] // CHUNK):
                sp.dma_start(s["in"][:, CHUNK * c:CHUNK * (c + 1), :],
                             s["slots"].rearrange("(t p) r -> p t r", p=P)[:, CHUNK * c:CHUNK * (c + 1), :])\
                    .then_inc(s["rows"], 16)
                sp.wait_ge(*s.at("rows", 16 * c + 16))
            for k in range(CHUNK):
                sp.wait_ge(scattered[k], 16 * (s["before"] + s["tiles"] // CHUNK))
            for b in range(B):
                tb = slice(NT // B * b, NT // B * (b + 1))
                for k in range(s["K"]):
                    y = s["ydram"][T * k:T * (k + 1)].rearrange("(t p) n -> p t n", p=P)
                    sp.dma_start(s["ybuf"][:, k, tb], y[:, tb]).then_inc(loaded[b], 16)

        def moe_pool(pool, s):
            pool.wait_ge(ld["pad"], s["pads"])
            cols = 1 if s["top2"] else 2
            for k in range(s["K"]):
                for t in range(NT):
                    g = t // (NT // B)
                    if t == 0 or (k == 1 and t % (NT // B) == 0):
                        pool.wait_ge(*s.at("cols", cols + k * (1 + g)))
                    nc.gpsimd.indirect_dma_start(
                        out=s["slots"], out_offset=bass.IndirectOffsetOnAxis(ap=slot_i[:, k, t:t + 1], axis=0),
                        in_=rows[:, t, :], in_offset=None).then_inc(s[f"sent{g}"], 16)
            with pool.Fori(0, s["tiles"] // CHUNK) as c:
                for k in range(CHUNK):
                    t = CHUNK * c + k
                    if k % 2 == 0:
                        pool.wait_ge(*s.at("y", CP * c + k // 2 + 1 + RING))
                        column = CP * c + k // 2 + CP * (s["before"] - 1)
                        nc.gpsimd.tensor_copy(pool_junk[:, ds(column, 1)], ones_bf[:, 0:1])
                    nc.gpsimd.indirect_dma_start(
                        out=s["ydram"], out_offset=bass.IndirectOffsetOnAxis(ap=out_idx[:, k:k + 1], axis=0),
                        in_=s["ysb"][:, k], in_offset=None).then_inc(scattered[k], 16)

        CH = NT // B
        HALF = P // 2

        gl = sems("gla", "q", "qcopied", "f", "fused", "a", "products", "inverses", "chain", "update", "dve", "scaled",
                  "st1", "act1", "am", "st2", "state", "act2", "y", "ycopied", "rs", "add")
        ga = {}
        ga["qT"] = arena[:, 0:4096]
        ga["f"] = arena[:, 4096:5120].rearrange("p (k n) -> p k n", k=2)
        ga["a"] = arena[:, 5120:6144].rearrange("p (k n) -> p k n", k=2)
        ga["c"] = arena[:, 6144:7168].rearrange("p (k n) -> p k n", k=2)
        ga["r"] = arena[:, 7168:8192].rearrange("p (k n) -> p k n", k=2)
        ga["k"] = arena[:, 8192:9216].rearrange("p (k n) -> p k n", k=2)
        for i, n in enumerate(("kt", "v", "am", "oT", "sq", "S", "tmp")):
            o = 9216 + 256 * i
            ga[n] = arena[:, o:o + 256].rearrange("p (k n) -> p k n", k=2)
        ga["zero"] = arena[:, 11008:11136]
        ga["ss"] = sb("gla_ss", [P, NT])
        gy = xn

        def gla_tensor(pe, ln):
            pe.wait_ge(*ln.at("copied", 2 * NS))
            pe.wait_ge(*ln.at("low", NS))
            pe.wait_ge(pr["gla"], 4)
            for i in range(NS):
                pe.wait_ge(gl["qcopied"], i + 1)
                nc.tensor.matmul(bank[i % 2][:], wqT[:], xnT[:, NMAX * i:NMAX * (i + 1)], start=True, stop=True)\
                    .then_inc(gl["q"], 1)
            A, KV, O, DS, Y, FB = (bank[0], bank[1]), (bank[2], bank[3]), bank[4], bank[5], bank[6], bank[7]
            pe.wait_ge(gl["qcopied"], NS + 2)

            def keys(half):
                pe.wait_ge(gl["fused"], half + 1)
                nc.tensor.matmul(FB[:], wkT[:], xnT[:, ds(NMAX * half, NMAX)], start=True, stop=True).then_inc(gl["f"], 1)

            def batch(b, last):

                def stage1(i):
                    n, k, c = CH * b + i, i // TPS, slice(P * (i % TPS), P * (i % TPS) + P)
                    tok = ds(2 * NMAX * b + P * i, P)
                    kv = KV[i % 2]
                    pe.wait_ge(gl["act1"], n + 1)
                    nc.tensor.matmul(kv[:, P:2 * P], xh[:, tok], wvh[:], start=True, stop=False)
                    nc.tensor.matmul(kv[:, P:2 * P], xl[:, tok], wvh[:], start=False, stop=False)
                    nc.tensor.matmul(kv[:, P:2 * P], xh[:, tok], wvl[:], start=False, stop=True)
                    pe.wait_ge(gl["scaled"], 2 * b + k + 3)
                    nc.tensor.transpose(kv[:, 0:P], ga["k"][:, k, c], ident)
                    pe.wait_ge(gl["am"], n + 1)
                    nc.tensor.matmul(A[i % 2][:, 0:P], ga["k"][:, k, c], ga["qT"][:, tok], start=True, stop=True)\
                        .then_inc(gl["st1"], 1)

                def stage2(i):
                    n = CH * b + i
                    tok = ds(2 * NMAX * b + P * i, P)
                    pe.wait_ge(gl["act1"], n + 3)
                    pe.wait_ge(gl["state"], n + 1)
                    nc.tensor.matmul(DS[:, 0:P], ga["kt"][:, i % 2], ga["v"][:, i % 2], start=True, stop=True)\
                        .then_inc(gl["update"], 1)
                    pe.wait_ge(gl["am"], n + 3)
                    pe.wait_ge(gl["act2"], n + 1)
                    nc.tensor.matmul(O[:, 0:P], ga["v"][:, i % 2], ga["am"][:, i % 2], start=True, stop=False)
                    state = ga["S"][:, i % 2] if i > 0 else ga["zero"]
                    nc.tensor.matmul(O[:, 0:P], state, ga["qT"][:, tok], start=False, stop=True).then_inc(gl["st2"], 1)

                def stage3(i):
                    n = CH * b + i
                    pe.wait_ge(gl["act2"], n + 2)
                    pe.wait_ge(gl["ycopied"], n + 1)
                    nc.tensor.matmul(Y[:, 0:P], ga["oT"][:, i % 2], woTn[:], start=True, stop=True)
                    nc.tensor.matmul(Y[:, P:P + 1], ga["sq"][:, i % 2], ones_f[:, 0:1], start=True, stop=True)\
                        .then_inc(gl["y"], 1)

                for i in range(CH + 2):
                    if i < CH:
                        stage1(i)
                    if 1 <= i <= CH:
                        stage2(i - 1)
                    if i >= 2:
                        stage3(i - 2)
                    if i in (2, 6) and not last:
                        keys(2 * b + 2 + i // 4)

            keys(0)
            keys(1)
            with pe.Fori(0, B - 1) as b:
                batch(b, False)
            batch(B - 1, True)

        def gla_scalar(act, ln):
            warm(act, ACT.Silu)
            for i in range(NS):
                act.wait_ge(gl["q"], i + 1)
                nc.scalar.activation(ga["qT"][:, NMAX * i:NMAX * (i + 1)], bank[i % 2][:], ACT.Silu)\
                    .then_inc(gl["qcopied"], 1)
            warm(act, ACT.Sigmoid)

            def decay(half, k):
                act.wait_ge(gl["f"], half + 1)
                act.wait_ge(gl["scaled"], half + 1)
                nc.scalar.activation(ga["f"][:, k], bank[7][:], ACT.Sigmoid).then_inc(gl["fused"], 1)
                act.wait_ge(gl["fused"], half + 2)
                nc.scalar.activation(ga["a"][:, k], ga["f"][:, k], ACT.Sigmoid).then_inc(gl["a"], 1)

            def batch(b, last):
                def copy1(i):
                    n = CH * b + i
                    act.wait_ge(gl["st1"], n + 1)
                    act.wait_ge(gl["st2"], n + 1)
                    nc.scalar.activation(ga["kt"][:, i % 2], bank[2 + i % 2][:, 0:P], ACT.Copy)
                    nc.scalar.activation(ga["v"][:, i % 2], bank[2 + i % 2][:, P:2 * P], ACT.Copy)\
                        .then_inc(gl["act1"], 1)

                def copy2(i):
                    n = CH * b + i
                    act.wait_ge(gl["st2"], n + 3)
                    act.wait_ge(gl["y"], n + 1)
                    nc.scalar.activation(ga["oT"][:, i % 2], bank[4][:, 0:P], ACT.Copy)
                    nc.scalar.activation(ga["sq"][:, i % 2], bank[4][:, 0:P], ACT.Square).then_inc(gl["act2"], 1)

                def copy3(i):
                    n = CH * b + i
                    act.wait_ge(gl["y"], n + 3)
                    nc.scalar.activation(gy[:, ds(n, 1), :], bank[6][:, 0:P].unsqueeze(1), ACT.Copy)
                    nc.scalar.activation(ga["ss"][:, ds(n, 1)], bank[6][:, P:P + 1], ACT.Copy)\
                        .then_inc(gl["ycopied"], 1)

                for i in range(CH + 2):
                    if i < CH:
                        copy1(i)
                    if 1 <= i <= CH:
                        copy2(i - 1)
                    if i >= 2:
                        copy3(i - 2)
                    if i in (2, 6) and not last:
                        decay(2 * b + 2 + i // 4, i // 4)

            decay(0, 0)
            decay(1, 1)
            with act.Fori(0, B - 1) as b:
                batch(b, False)
            batch(B - 1, True)

        def gla_pool(pool):
            c, r, f, kn = (ga[n] for n in ("c", "r", "f", "k"))
            for b in range(B):
                for k in range(2):
                    half = 2 * b + k
                    q = ga["qT"][:, NMAX * half:NMAX * (half + 1)]
                    pool.wait_ge(gl["products"], half + 1)
                    nc.gpsimd.tensor_tensor(q, q, c[:, k], ALU.mult).then_inc(gl["chain"], 1)
                    nc.gpsimd.tensor_scalar(kn[:, k], f[:, k], 1.0, 1.0, ALU.subtract, ALU.mult).then_inc(gl["chain"], 1)
                    pool.wait_ge(gl["inverses"], half + 1)
                    pool.wait_ge(gl["chain"], 3 * half + 2)
                    nc.gpsimd.tensor_tensor(kn[:, k], kn[:, k], r[:, k], ALU.mult).then_inc(gl["chain"], 1)
                    pool.wait_ge(gl["chain"], 3 * half + 3)
                    first = lambda v: v.rearrange("p (j h f) -> p j h f", h=2, f=HALF)[:, :, 0]
                    middle = lambda v: first(v)[:, :, HALF - 1:HALF].to_broadcast([P, TPS, HALF])
                    q1, k1 = first(q), first(kn[:, k])
                    nc.gpsimd.tensor_tensor(q1, q1, middle(r[:, k]), ALU.mult)
                    nc.gpsimd.tensor_tensor(k1, k1, middle(c[:, k]), ALU.mult).then_inc(gl["scaled"], 1)

        def gla_vector(dve, ln):
            for i, (q, v) in enumerate((("qcopied", 2), ("fused", 1), ("scaled", 2), ("act1", 2), ("am", 2), ("state", 1),
                                        ("act2", 1), ("st2", 2), ("y", 2), ("ycopied", 1))):
                nc.vector.memset(credit[:, i:i + 1], 0.0).then_inc(gl[q], v)
            c, r, a = (ga[n] for n in ("c", "r", "a"))
            for ap in (ga["zero"], ga["am"]):
                last = nc.vector.memset(ap, 0.0)
            last.then_inc(pr["gla"], 1)
            dve.wait_ge(ld["gla"], LD_GLA)
            nc.vector.tensor_copy(wvh[:], wvT[:]).then_inc(pr["gla"], 1)
            dve.wait_ge(pr["gla"], 2)
            nc.vector.tensor_tensor(wvl[:], wvT[:], wvh[:], ALU.subtract).then_inc(pr["gla"], 1)
            nc.vector.tensor_scalar(woTn[:], woT[:], normw[:, 0:1], None, ALU.mult).then_inc(pr["gla"], 1)

            def products(half, k, states):
                dve.wait_ge(gl["a"], half + 1)
                dve.wait_ge(gl["state"], states)
                for h in range(NMAX // HALF):
                    seg = slice(HALF * h, HALF * h + HALF)
                    last = nc.vector.tensor_tensor_scan(c[:, k, seg], a[:, k, seg], ga["zero"][:, 0:HALF], 1.0,
                                                        ALU.mult, ALU.add)
                last.then_inc(gl["products"], 1)

            def inverses(half, k):
                dve.wait_ge(gl["products"], half + 1)
                nc.vector.reciprocal(r[:, k], c[:, k]).then_inc(gl["inverses"], 1)

            def batch(b, last):
                def mask(i):
                    n = CH * b + i
                    A, am = bank[i % 2], ga["am"][:, i % 2]
                    dve.wait_ge(gl["st1"], n + 1)
                    dve.wait_ge(gl["st2"], n + 1)
                    nc.vector.tensor_tensor(am[0:HALF], A[0:HALF, 0:P], negmask[0:HALF], ALU.mult)
                    nc.vector.tensor_tensor(am[HALF:P, HALF:P], A[HALF:P, HALF:P], negmask[HALF:P, HALF:P],
                                            ALU.mult).then_inc(gl["am"], 1)

                def state(i):
                    n = CH * b + i
                    e2 = c[:, i // TPS, P * (i % TPS) + P - 1:P * (i % TPS) + P]
                    nx = min(i + 1, CH - 1)
                    e1 = c[:, nx // TPS, P * (nx % TPS) + HALF - 1:P * (nx % TPS) + HALF]
                    cur = ga["S"][:, i % 2] if i > 0 else ga["zero"]
                    dve.wait_ge(gl["update"], n + 1)
                    dve.wait_ge(gl["state"], n + 1)
                    nc.vector.tensor_tensor(ga["tmp"][:, i % 2], cur, bank[5][:, 0:P], ALU.subtract).then_inc(gl["dve"], 1)
                    dve.wait_ge(gl["dve"], n + 1)
                    dve.wait_ge(gl["st2"], n + 2)
                    nc.vector.tensor_scalar(ga["S"][:, (i + 1) % 2], ga["tmp"][:, i % 2], e2, e1, ALU.mult, ALU.mult)\
                        .then_inc(gl["state"], 1)

                for i in range(CH + 1):
                    if i < CH:
                        mask(i)
                    if i >= 1:
                        state(i - 1)
                    if i == CH or (last and i >= 4):
                        continue
                    half, k = 2 * b + 1 + i // 4, (1 + i // 4) % 2
                    if i % 4 == 0:
                        products(half, k, CH * b + i + 1)
                    elif i % 4 == 1:
                        inverses(half, k)

            products(0, 0, 1)
            inverses(0, 0)
            with dve.Fori(0, B - 1) as b:
                batch(b, False)
            batch(B - 1, True)
            ms, rs = nwt[:, 0, :], nwt[:, 5, :]
            dve.wait_ge(gl["ycopied"], NT + 1)
            nc.vector.tensor_scalar(ms, ga["ss"][:], 1.0 / P, 1e-6, ALU.mult, ALU.add).then_inc(gl["rs"], 1)
            dve.wait_ge(gl["rs"], 1)
            inverse_sqrt(dve, gl["rs"], 1, ms, rs)
            for t in range(NT):
                nc.vector.scalar_tensor_tensor(x[:, t, :], gy[:, t, :], rs[:, t:t + 1], x[:, t, :], ALU.mult, ALU.add)\
                    .then_inc(gl["add"], 1)

        NJ = L // P
        au = sems("gau", "b", "bs", "uvp", "uv", "qkp", "qkc", "dve", "z", "zt", "ztc", "o", "add", "rb")
        uv = arena[:, 0:4096].rearrange("p (k n f) -> p k n f", k=2, n=B)
        qk = arena[:, 4096:6144].rearrange("p (k n f) -> p k n f", k=2, n=B)
        bs = arena[:, 6144:7168].rearrange("p (k f) -> p k f", k=2)
        z = arena[:, 7168:9216].rearrange("p (k n f) -> p k n f", k=2, n=B)
        zT = arena[:, 9216:10240].rearrange("p (n c f) -> p n c f", n=B, c=2)
        junk = arena[:, 10240:11520].rearrange("p (a f) -> p a f", a=10)
        x2n = arena[:, 0:4096].rearrange("p (t f) -> p t f", f=P)
        kern = sb("kern", [P, 4, 10])
        OFF = [0, 1, 3, 6]

        def gau_pool(pool, ln):
            pool.wait_ge(ld["gau"], LD_GAU)
            for n in range(B):
                for i in range(2):
                    nc.gpsimd.tensor_scalar(rotqk[:, n, P * i:P * i + P], rot[:, n, :], cols[:, 3 + i:4 + i], 0.0,
                                            ALU.mult, ALU.add).then_inc(pr["gau"], 1)
                nc.gpsimd.tensor_copy(bias10[:, OFF[n]:OFF[n] + n + 1], wrel[:, 3 - n:4]).then_inc(pr["gau"], 1)
            nc.gpsimd.tensor_copy(wuvh[:], wuv[:]).then_inc(pr["gau"], 1)
            pool.wait_ge(pr["gau"], 13)
            nc.gpsimd.tensor_tensor(wuvl[:], wuv[:], wuvh[:], ALU.subtract).then_inc(pr["gau"], 1)

        def gau_shortcut(pool, ln):
            pool.wait_ge(*ln.at("norm", NT))
            nc.gpsimd.tensor_tensor(x[:], x[:], xn[:], ALU.add).then_inc(pr["gau_mm"], 1)
            pool.wait_ge(pr["gau_mm"], 1)
            nc.gpsimd.tensor_tensor(x[:], x[:], bo_b[:].unsqueeze(1).to_broadcast([P, NT, P]), ALU.add)\
                .then_inc(pr["gau_mm"], 1)

        def gau_tensor(pe, ln):
            pe.wait_ge(pr["gau"], 14)
            for n in range(B):
                for i in range(2):
                    last = nc.tensor.matmul(bank[2 + n // 2][0:1, 256 * (n % 2) + P * i:256 * (n % 2) + P * i + P],
                                            cols[:, 5 + i:6 + i], rot[:, n, :], start=True, stop=True)
            last.then_inc(au["rb"], 1)
            pe.wait_ge(*ln.at("low", NS))

            def front(j, par):
                pe.wait_ge(au["bs"], j + 1)
                xs = xnT.rearrange("p (n j f) -> p j n f", n=B, f=P)[:, ds(j, 1)]
                nc.tensor.matmul(bank[0][:], wbT[:], xs, start=True, stop=True).then_inc(au["b"], 1)
                for n in range(B):
                    ps = bank[1 + n % 2][:]
                    tok = ds(P * j + L * n, P)
                    pe.wait_ge(au["uv"], B * j + n + 1)
                    nc.tensor.matmul(ps, ones_bf[0:BR, 0:P], uvrows[:], start=True, stop=False)
                    nc.tensor.matmul(ps, xh[:, tok], wuvh[:], start=False, stop=False)
                    nc.tensor.matmul(ps, xl[:, tok], wuvh[:], start=False, stop=False)
                    nc.tensor.matmul(ps, xh[:, tok], wuvl[:], start=False, stop=True).then_inc(au["uvp"], 1)
                pe.wait_ge(au["bs"], j + 2)
                for n in range(B):
                    if n % 2 == 0:
                        pe.wait_ge(au["qkc"], 2 * j + n // 2 + 1)
                    ps = bank[3 + n // 2][:, 256 * (n % 2):256 * (n % 2) + 256]
                    nc.tensor.matmul(ps, ones_f[0:1, :], rotb[:, n, :], start=True, stop=False)
                    last = nc.tensor.matmul(ps, bs[:, par, P * n:P * n + P], rotqk[:, n, :], start=False, stop=True)
                    if n % 2:
                        last.then_inc(au["qkp"], 1)

            def back(j, par):
                pe.wait_ge(au["z"], j + 3)
                pe.wait_ge(au["ztc"], j + 1)
                for n in range(B):
                    for c in range(2):
                        o = 256 * (n % 2) + P * c
                        last = nc.tensor.transpose(bank[5 + n // 2][:, o:o + P], z[:, par, n, P * c:P * c + P], ident)
                last.then_inc(au["zt"], 1)
                pe.wait_ge(au["ztc"], j + 2)
                pe.wait_ge(au["add"], j + 1)
                for n in range(B):
                    for c in range(2):
                        last = nc.tensor.matmul(bank[7][:, P * n:P * n + P], zT[:, n, c], wo1[:, c, :],
                                                start=(c == 0), stop=(c == 1))
                last.then_inc(au["o"], 1)

            pe.wait_ge(au["rb"], 3)
            front(0, 0)
            with pe.Fori(0, NJ // 2 - 1) as pair:
                j = 2 * pair
                front(j + 1, 1)
                back(j, 0)
                front(j + 2, 0)
                back(j + 1, 1)
            front(NJ - 1, 1)
            back(NJ - 2, 0)
            back(NJ - 1, 1)

        def gau_scalar(act, ln):
            warm(act, ACT.Silu)
            act.wait_ge(au["rb"], 1)
            for i in range(2):
                nc.scalar.activation(rotb[:, 2 * i:2 * i + 2, :], bank[2 + i][0:1, :].rearrange("p (a f) -> p a f", a=2),
                                     ACT.Copy).then_inc(au["rb"], 1)

            def front(j, par):
                act.wait_ge(au["b"], j + 1)
                nc.scalar.activation(bs[:, par], bank[0][:], ACT.Silu, bias=cols[:, 2:3]).then_inc(au["bs"], 1)
                act.wait_ge(au["z"], j + 1)
                for n in range(B):
                    act.wait_ge(au["uvp"], B * j + n + 1)
                    nc.scalar.activation(uv[:, par, n], bank[1 + n % 2][:], ACT.Silu).then_inc(au["uv"], 1)
                for h in range(2):
                    act.wait_ge(au["qkp"], 2 * j + h + 1)
                    nc.scalar.activation(qk[:, par, 2 * h:2 * h + 2], bank[3 + h][:].rearrange("p (a f) -> p a f", a=2),
                                         ACT.Copy).then_inc(au["qkc"], 1)

            def back(j, par):
                act.wait_ge(au["zt"], j + 3)
                act.wait_ge(au["o"], j + 1)
                for h in range(2):
                    last = nc.scalar.activation(zT[:, 2 * h:2 * h + 2],
                                                bank[5 + h][:].rearrange("p (a c f) -> p a c f", a=2, c=2), ACT.Copy)
                last.then_inc(au["ztc"], 1)

            front(0, 0)
            with act.Fori(0, NJ // 2 - 1) as pair:
                j = 2 * pair
                front(j + 1, 1)
                back(j, 0)
                front(j + 2, 0)
                back(j + 1, 1)
            front(NJ - 1, 1)
            back(NJ - 2, 0)
            back(NJ - 1, 1)

        def gau_vector(dve, ln):
            for i, (q, v) in enumerate((("bs", 1), ("uv", 2), ("qkc", 2), ("z", 2), ("ztc", 1), ("add", 1),
                                        ("zt", 2), ("o", 1))):
                nc.vector.memset(credit[:, 16 + i:17 + i], 0.0).then_inc(au[q], v)
            dve.wait_ge(pr["gau_mm"], 2)
            qk10, t, r, kk = (kern[:, i, :] for i in range(4))
            STEPS = 9

            def front(j, par):
                at = j * STEPS
                dve.wait_ge(au["qkc"], 2 * j + 4)
                for n in range(B):
                    for m in range(n + 1):
                        i = OFF[n] + m
                        last = nc.vector.tensor_tensor_reduce(
                            out=junk[:, i], in0=qk[:, par, n, 0:P], in1=qk[:, par, m, P:2 * P], scale=1.0, scalar=0.0,
                            op0=ALU.mult, op1=ALU.add, accum_out=qk10[:, i:i + 1])
                last.then_inc(au["dve"], 1)
                dve.wait_ge(au["dve"], at + 1)
                nc.vector.scalar_tensor_tensor(t, qk10, 1.0 / 64, bias10[:], ALU.mult, ALU.add).then_inc(au["dve"], 1)
                dve.wait_ge(au["dve"], at + 2)
                nc.vector.tensor_scalar(r, t, 0.0, None, ALU.max).then_inc(au["dve"], 1)
                dve.wait_ge(au["dve"], at + 3)
                nc.vector.tensor_tensor(kk, r, r, ALU.mult).then_inc(au["dve"], 1)
                dve.wait_ge(au["dve"], at + 4)
                dve.wait_ge(au["uv"], B * j + B + 2)
                dve.wait_ge(au["zt"], j + 1)
                for m in range(B):
                    for n in range(m, B):
                        i = OFF[n] + m
                        v, w, zn = uv[:, par, m, 0:EH], kk[:, i:i + 1], z[:, par, n]
                        if m == 0:
                            last = nc.vector.tensor_scalar(zn, v, w, None, ALU.mult)
                        else:
                            last = nc.vector.scalar_tensor_tensor(zn, v, w, zn, ALU.mult, ALU.add)
                    last.then_inc(au["dve"], 1)
                    dve.wait_ge(au["dve"], at + 5 + m)
                nc.vector.tensor_tensor(z[:, par], z[:, par], uv[:, par, :, EH:2 * EH], ALU.mult).then_inc(au["z"], 1)
                nc.vector.memset(credit[:, 31:32], 0.0).then_inc(au["dve"], 1)
                dve.wait_ge(au["dve"], at + 9)

            def back(j, par):
                dve.wait_ge(au["o"], j + 2)
                xj = x[:].rearrange("p (n j) f -> p j n f", n=B)[:, ds(j, 1)]
                nc.vector.tensor_tensor(xj, xj, bank[7][:].rearrange("p (j n f) -> p j n f", j=1, n=B), ALU.add)\
                    .then_inc(au["add"], 1)

            front(0, 0)
            with dve.Fori(0, NJ // 2 - 1) as pair:
                j = 2 * pair
                front(j + 1, 1)
                back(j, 0)
                front(j + 2, 0)
                back(j + 1, 1)
            front(NJ - 1, 1)
            back(NJ - 2, 0)
            back(NJ - 1, 1)

        W0 = dict(FC=FC0, w1=(w1h0, w1l0), w2=(w2h0, w2l0), wr=wr0[:], bias=False, top2=False)
        W1 = dict(FC=FC1, w1=(w1h1, w1l1), w2=(w2h1, w2l1), wr=wr1[:], bias=True, top2=True)
        moe_done = lambda s: [s.at("comb", B)]
        xg, xb = cols[:, 0:1], cols[:, 1:2]

        ln0 = layernorm(x, xn, [(loaded[b], 16) for b in range(B)], halves=False)
        moe0 = moe("moe0", ln0, 0, **W0)
        ln1 = layernorm(x, xn, moe_done(moe0))
        ln2 = layernorm(x, xn, [(gl["add"], NT)], halves=False)
        moe2 = moe("moe2", ln2, 1, **W0)
        ln3 = layernorm(x, xn, moe_done(moe2), halves=False)
        moe3 = moe("moe3", ln3, 2, **W1)
        ln4 = layernorm(x, xn, moe_done(moe3), halves=False, turn=False)
        ln5 = layernorm(xn, x2n, [ln4.at("norm", NT)], (xg, xb))
        ln6 = layernorm(x, xn, [(au["add"], NJ + 1)], halves=False)
        moe6 = moe("moe6", ln6, 3, **W1)
        stored = sem("stored")

        @block.sync
        def _(sp):
            load_sync(sp)
            moe_sync(sp, moe0, [(pr["w0l"], 2)])
            load_pads(sp)
            moe_sync(sp, moe2)
            moe_sync(sp, moe3)
            moe_sync(sp, moe6)
            for b in range(B):
                sp.wait_ge(*moe6.at("comb", b + 1))
                sp.dma_start(out[b].rearrange("(a p) n -> p a n", p=P), x[:, NT // B * b:NT // B * (b + 1)])\
                    .then_inc(stored, 16)
            sp.wait_ge(stored, 16 * B)
        @block.gpsimd
        def _(pool):
            nc.gpsimd.memset(ones_bf[:], 1.0).then_inc(pr["pool"], 1)
            nc.gpsimd.memset(ones_f[:], 1.0).then_inc(pr["pool"], 1)
            nc.gpsimd.memset(eps[:], 0.5).then_inc(pr["pool"], 1)
            for e in range(E):
                pool.dma_start(st_w2_0[:, e], d["w2_0"][e].rearrange("(c p) n -> p c n", p=P)).then_inc(scattered[e], 16)
            pool.wait_ge(ld["consts"], 32)
            nc.gpsimd.tensor_copy(strict_bf[:], consts[:, C_STRICT:C_STRICT + P]).then_inc(pr["pool"], 1)
            nc.gpsimd.tensor_copy(ident_bf[:], ident).then_inc(pr["pool"], 1)
            for i, (st, hi, lo, q, v) in enumerate(((st_w1_1, w1h1, w1l1, ld["w1"], LD_W1),
                                                    (st_w2_1, w2h1, w2l1, ld["w1b"], 16 * E))):
                pool.wait_ge(q, v)
                nc.gpsimd.tensor_copy(hi[:], st).then_inc(pr["w1h"], 1)
                pool.wait_ge(pr["w1h"], i + 1)
                nc.gpsimd.tensor_tensor(lo[:], st, hi[:], ALU.subtract).then_inc(pr["w1l"], 1)
            moe_pool(pool, moe0)
            gla_pool(pool)
            rows_pool(pool)
            gau_pool(pool, ln4)
            moe_pool(pool, moe2)
            moe_pool(pool, moe3)
            gau_shortcut(pool, ln4)
            moe_pool(pool, moe6)

        @block.vector
        def _(dve):
            for b in range(B):
                dve.wait_ge(loaded[b], 16)
                ln_stats(ln0, range(NT // B * b, NT // B * (b + 1)))
            ln0["begun"] = True
            ln_vector(dve, ln0)

            def low_halves():
                dve.wait_ge(pr["w0h"], 2)
                nc.vector.tensor_tensor(w1l0[:], st_w1_0, w1h0[:], ALU.subtract).then_inc(pr["w0l"], 1)
                nc.vector.tensor_tensor(w2l0[:], st_w2_0, w2h0[:], ALU.subtract).then_inc(pr["w0l"], 1)
                dve.wait_ge(pr["w0l"], 2)
            moe_vector(dve, moe0, low_halves, next_ln=ln1)
            ln_vector(dve, ln1)
            dve.wait_ge(pr["w1l"], 2)
            gla_vector(dve, ln1)
            ln_vector(dve, ln2)
            dve.wait_ge(pr["rows"], ROWS_DONE)
            moe_vector(dve, moe2, next_ln=ln3)
            ln_vector(dve, ln3)
            moe_vector(dve, moe3, next_ln=ln4)
            ln_vector(dve, ln4)
            ln_vector(dve, ln5)
            gau_vector(dve, ln5)
            ln_vector(dve, ln6)
            moe_vector(dve, moe6)

        @block.scalar
        def _(act):
            act.wait_ge(pr["pool"], 5)
            ln_scalar(act, ln0)

            def high_halves():
                act.wait_ge(ld["w0"], LD_W0)
                for e in range(E):
                    act.wait_ge(scattered[e], 16)
                nc.scalar.activation(w1h0[:], st_w1_0, ACT.Copy).then_inc(pr["w0h"], 1)
                nc.scalar.activation(w2h0[:], st_w2_0, ACT.Copy).then_inc(pr["w0h"], 1)
            moe_scalar(act, moe0, high_halves)
            ln_scalar(act, ln1)
            gla_scalar(act, ln1)
            ln_scalar(act, ln2)
            moe_scalar(act, moe2)
            ln_scalar(act, ln3)
            moe_scalar(act, moe3)
            act.wait_ge(ld["gau"], LD_GAU)
            ln_scalar(act, ln5)
            gau_scalar(act, ln5)
            ln_scalar(act, ln6)
            moe_scalar(act, moe6)

        @block.tensor
        def _(pe):
            pe.wait_ge(ld["consts"], 32)
            moe_tensor(pe, moe0, [(pr["w0l"], 2)])
            ln_tensor(pe, ln1)
            gla_tensor(pe, ln1)
            moe_tensor(pe, moe2)
            pe.wait_ge(pr["w1l"], 2)
            pe.wait_ge(ld["w1"], LD_W1)
            pe.wait_ge(pr["rows"], ROWS_DONE)
            moe_tensor(pe, moe3)
            ln_tensor(pe, ln5)
            gau_tensor(pe, ln5)
            moe_tensor(pe, moe6)


def kernel(**inputs):
    import numpy as np
    import concourse.bacc as bacc
    from concourse.bass_utils import run_bass_kernel_spmd as run

    a = {k: np.asarray(v) for k, v in inputs.items()}
    c = np.ascontiguousarray
    f = np.float32
    k = np.arange(P)
    consts = np.zeros((P, C_END), f)
    consts[:, C_IDENT:C_IDENT + P] = np.eye(P, dtype=f)
    consts[:, C_NEGMASK:C_NEGMASK + P] = -(k[:, None] <= k[None, :]).astype(f)
    consts[:, C_STRICT:C_STRICT + P] = (k[:, None] < k[None, :]).astype(f)
    consts[:, C_SAMEEXP:C_SAMEEXP + P] = (k[:, None] % E == k[None, :] % E).astype(f)
    consts[:, C_RANK:C_RANK + E] = (E - np.arange(E)).astype(f)[None]
    consts[:, C_RESET:C_RESET + 256] = (np.arange(256) % 32 != 0).astype(f)[None]
    half = P // 2
    inv = (f(10000.0) ** (-np.arange(half, dtype=f) / f(half))).astype(f)
    rot = np.zeros((P, 4, P), f)
    i = np.arange(half)
    for n in range(4):
        ang = (f(n) * inv).astype(f)
        s, co = np.sin(ang).astype(f), np.cos(ang).astype(f)
        rot[i, n, i] = co
        rot[i + half, n, i] = -s
        rot[i + half, n, i + half] = co
        rot[i, n, i + half] = s
    T = a['L0_attn_x'].shape[0] * a['L0_attn_x'].shape[1]
    NT = T // P
    dest = (k[:, None, None] + P * np.arange(NT)[None, None] + T * np.arange(2)[None, :, None]).astype(np.int32)

    def pad(choices):
        n = (choices * NT + 2 * E) * P
        r = np.zeros((n, P + 2), f)
        r[:, P] = (choices * T + np.arange(n, dtype=np.int32)).view(f)
        return r

    uv = np.concatenate([a['L1_attn_bv'], a['L1_attn_bu']])
    brows = np.concatenate([a['L1_ffn_b2'], a['L1_ffn_b1'], np.zeros((E, uv.shape[0]), f)], 1)
    brows[0, -uv.shape[0]:] = uv
    F1 = a['L1_ffn_W1'].shape[2]
    selector = np.zeros((3, 32, E, F1), np.uint16)
    for e in range(E):
        selector[:, e, e] = 0x3f80
    selector = selector.reshape(96, E * F1)
    centre = a['L1_attn_w_rel'].shape[0] // 2
    arrays = {
        "x": a['L0_attn_x'], "consts": consts, "wg": a['L0_ffn_Wg'], "w1_0": a['L0_ffn_W1'], "w2_0": a['L0_ffn_W2'],
        "wqT": a['L0_attn_Wq'].T, "wkT": a['L0_attn_Wk'].T, "wvT": a['L0_attn_Wv'].T, "woT": a['L0_attn_Wo'].T,
        "norm_w": a['L0_attn_norm_w'][:, None],
        "w1_1": a['L1_ffn_W1'], "w2_1": a['L1_ffn_W2'], "wrT": a['L1_ffn_Wr'].T,
        "brows": brows, "selector": selector,
        "dest": dest, "starts": np.stack([2 * P * np.arange(NT + E), 8 ** (np.arange(NT + E) % 8)]).astype(f)[None], "pad1": pad(1), "pad2": pad(2),
        "wvT1": a['L1_attn_Wv'].T, "wuT": a['L1_attn_Wu'].T, "wbT": a['L1_attn_Wb'].T,
        "cols": np.stack([a['L1_attn_' + n] for n in ('ln_g', 'ln_b', 'bb', 'qqw', 'qkw', 'qqb', 'qkb')], 1),
        "rot": rot, "wo1": a['L1_attn_Wo'].T.reshape(2, P, P).transpose(1, 0, 2),
        "wrel": a['L1_attn_w_rel'][centre - 3:centre + 1], "bo": a['L1_attn_bo'],
    }
    nc = bacc.Bacc("TRN2", target_bir_lowering=False, num_devices=1)
    feed, d = {}, {}
    for name, v in arrays.items():
        v = c(v)
        feed[f"in_{name}"] = v
        d[name] = nc.dram_tensor(f"in_{name}", v.shape, mybir.dt.from_np(v.dtype), kind="ExternalInput").ap()
    shape = arrays["x"].shape
    out = nc.dram_tensor("out_x", shape, F32, kind="ExternalOutput").ap()
    program(nc, d, out)
    return run(nc, [feed], core_ids=[0]).results[0]["out_x"]
```
